# Optimizing a Trainium2 kernel written in Bass

```python
import numpy as np
import jax
import jax.numpy as jnp

def _softmax(x, axis=-1):
    return jax.nn.softmax(x, axis=axis)

def _gelu(x):
    return jax.nn.gelu(x, approximate=True)

def _silu(x):
    return jax.nn.silu(x)

def _sigmoid(x):
    return jax.nn.sigmoid(x)

def _layernorm(x, axis=-1, eps=1e-05):
    m = jnp.mean(x, axis=axis, keepdims=True)
    v = jnp.var(x, axis=axis, keepdims=True)
    return (x - m) / jnp.sqrt(v + eps)

def _scatter_add(tgt, idx, src, axis=0):
    return tgt.at[idx].add(src)

def _segment_sum(src, seg, n):
    return jax.ops.segment_sum(src, seg, n)
kernel_name = 'mk_seq_postln_d1_jaxref_r8_99d7b2'

def setup_inputs(seed: int=0):
    np.random.seed(seed)
    _w = jnp.asarray

    def _L0_attn_setup():
        import jax, jax.numpy as jnp
        import numpy as np
        DIM = 128
        NUM_HEADS = 16
        HD = DIM // NUM_HEADS
        ROPE_DIM = 64
        ROPE_BASE = 10000.0

        def _apply_rope(t):
            D = t.shape[-1]
            N = t.shape[2]
            pos = jnp.arange(N, dtype=t.dtype)
            inv = 1.0 / ROPE_BASE ** (jnp.arange(0, D, 2, dtype=t.dtype) / D)
            freqs = pos[:, None] * inv[None, :]
            cos = jnp.cos(freqs)[None, None]
            sin = jnp.sin(freqs)[None, None]
            e = t[..., 0::2]
            o = t[..., 1::2]
            eo = e * cos - o * sin
            oo = e * sin + o * cos
            return jnp.stack([eo, oo], axis=-1).reshape(t.shape)
        key = jax.random.key(seed)
        ks = jax.random.split(key, 5)
        B, N = (2, 256)
        s = 0.02
        return {'x': jax.random.normal(ks[0], (B, N, DIM), dtype=jnp.float32), 'qkv_w': jax.random.normal(ks[1], (3 * DIM, DIM), dtype=jnp.float32) * s, 'qkv_b': jax.random.normal(ks[2], (3 * DIM,), dtype=jnp.float32) * s, 'proj_w': jax.random.normal(ks[3], (DIM, DIM), dtype=jnp.float32) * s, 'proj_b': jax.random.normal(ks[4], (DIM,), dtype=jnp.float32) * s}
    _L0_attn_in = _L0_attn_setup()

    def _L0_ffn_setup():
        import jax, jax.numpy as jnp
        import numpy as np
        B, T, C, H, E, K, F = (2, 256, 128, 16, 8, 2, 256)
        EPS = 1e-05

        def layernorm(x, w):
            m = x.mean(-1, keepdims=True)
            v = x.var(-1, keepdims=True)
            return (x - m) * jax.lax.rsqrt(v + EPS) * w

        def attention(x, c_attn_w, c_proj_w):
            b, t, c = x.shape
            hd = c // H
            q, k, v = jnp.split(x @ c_attn_w, 3, axis=-1)
            q = q.reshape(b, t, H, hd).transpose(0, 2, 1, 3)
            k = k.reshape(b, t, H, hd).transpose(0, 2, 1, 3)
            v = v.reshape(b, t, H, hd).transpose(0, 2, 1, 3)
            att = jnp.einsum('bhqd,bhkd->bhqk', q, k) / jnp.sqrt(jnp.asarray(hd, x.dtype))
            causal = jnp.tril(jnp.ones((t, t), bool))
            att = jnp.where(causal, att, jnp.asarray(-jnp.inf, att.dtype))
            att = jax.nn.softmax(att, axis=-1)
            y = jnp.einsum('bhqk,bhkd->bhqd', att, v)
            y = y.transpose(0, 2, 1, 3).reshape(b, t, c)
            return y @ c_proj_w

        def moe_mlp(x, router_w, w1, w2):
            b, t, c = x.shape
            xf = x.reshape(-1, c)
            router_logits = xf @ router_w
            probs = jax.nn.softmax(router_logits.astype(jnp.float32), axis=-1)
            rw, sel = jax.lax.top_k(probs, K)
            rw = rw / rw.sum(axis=-1, keepdims=True)
            rw = rw.astype(x.dtype)
            w1e = w1.reshape(c, E, F).transpose(1, 0, 2)
            w2e = w2.reshape(E, F, c)
            h = jax.nn.gelu(jnp.einsum('nc,ecf->enf', xf, w1e), approximate=False)
            y_all = jnp.einsum('enf,efc->nec', h, w2e)
            y_sel = jnp.take_along_axis(y_all, sel[:, :, None], axis=1)
            y = (y_sel * rw[:, :, None]).sum(axis=1)
            return y.reshape(b, t, c)
        key = jax.random.key(seed)
        ks = jax.random.split(key, 6)
        s = 0.02
        return {'x': jax.random.normal(ks[0], (B, T, C), jnp.float32), 'ln1_w': jnp.ones((C,), jnp.float32), 'c_attn_w': jax.random.normal(ks[1], (C, 3 * C), jnp.float32) * s, 'c_proj_w': jax.random.normal(ks[2], (C, C), jnp.float32) * s, 'ln2_w': jnp.ones((C,), jnp.float32), 'router_w': jax.random.normal(ks[3], (C, E), jnp.float32) * s, 'w1': jnp.clip(jax.random.normal(ks[4], (C, E * F), jnp.float32) * s, -0.06, 0.06), 'w2': jnp.clip(jax.random.normal(ks[5], (E * F, C), jnp.float32) * s, -0.06, 0.06)}
    _L0_ffn_in = _L0_ffn_setup()
    _d = {'L0_attn_x': _L0_attn_in['x'], 'L0_attn_qkv_w': _L0_attn_in['qkv_w'], 'L0_attn_qkv_b': _L0_attn_in['qkv_b'], 'L0_attn_proj_w': _L0_attn_in['proj_w'], 'L0_attn_proj_b': _L0_attn_in['proj_b'], 'L0_ffn_ln1_w': _L0_ffn_in['ln1_w'], 'L0_ffn_c_attn_w': _L0_ffn_in['c_attn_w'], 'L0_ffn_c_proj_w': _L0_ffn_in['c_proj_w'], 'L0_ffn_ln2_w': _L0_ffn_in['ln2_w'], 'L0_ffn_router_w': _L0_ffn_in['router_w'], 'L0_ffn_w1': _L0_ffn_in['w1'], 'L0_ffn_w2': _L0_ffn_in['w2']}
    _x0 = _d['L0_attn_x']
    _d['L0_attn_x'] = jax.random.normal(jax.random.fold_in(jax.random.key(seed), 1), (32, 256, 128), dtype=_x0.dtype)
    del _x0
    return _d

def reference(L0_attn_x, L0_attn_qkv_w, L0_attn_qkv_b, L0_attn_proj_w, L0_attn_proj_b, L0_ffn_ln1_w, L0_ffn_c_attn_w, L0_ffn_c_proj_w, L0_ffn_ln2_w, L0_ffn_router_w, L0_ffn_w1, L0_ffn_w2):

    def _L0_attn_ref(x, qkv_w, qkv_b, proj_w, proj_b):
        import jax, jax.numpy as jnp
        import numpy as np
        DIM = 128
        NUM_HEADS = 16
        HD = DIM // NUM_HEADS
        ROPE_DIM = 64
        ROPE_BASE = 10000.0

        def _apply_rope(t):
            D = t.shape[-1]
            N = t.shape[2]
            pos = jnp.arange(N, dtype=t.dtype)
            inv = 1.0 / ROPE_BASE ** (jnp.arange(0, D, 2, dtype=t.dtype) / D)
            freqs = pos[:, None] * inv[None, :]
            cos = jnp.cos(freqs)[None, None]
            sin = jnp.sin(freqs)[None, None]
            e = t[..., 0::2]
            o = t[..., 1::2]
            eo = e * cos - o * sin
            oo = e * sin + o * cos
            return jnp.stack([eo, oo], axis=-1).reshape(t.shape)
        B, N, C = x.shape
        H, D = (NUM_HEADS, HD)
        scale = D ** (-0.5)
        qkv = x @ qkv_w.T + qkv_b
        qkv = qkv.reshape(B, N, 3, H, D).transpose(2, 0, 3, 1, 4)
        q, k, v = (qkv[0], qkv[1], qkv[2])
        q = jnp.concatenate([_apply_rope(q[..., :ROPE_DIM]), q[..., ROPE_DIM:]], axis=-1)
        k = jnp.concatenate([_apply_rope(k[..., :ROPE_DIM]), k[..., ROPE_DIM:]], axis=-1)
        attn = jnp.einsum('bhnd,bhmd->bhnm', q, k) * scale
        attn = jax.nn.softmax(attn, axis=-1)
        out = jnp.einsum('bhnm,bhmd->bhnd', attn, v)
        out = out.transpose(0, 2, 1, 3).reshape(B, N, C)
        return out @ proj_w.T + proj_b

    def _L0_ffn_ref(x, ln1_w, c_attn_w, c_proj_w, ln2_w, router_w, w1, w2):
        import jax, jax.numpy as jnp
        import numpy as np
        B, T, C, H, E, K, F = (2, 256, 128, 16, 8, 2, 256)
        EPS = 1e-05

        def layernorm(x, w):
            m = x.mean(-1, keepdims=True)
            v = x.var(-1, keepdims=True)
            return (x - m) * jax.lax.rsqrt(v + EPS) * w

        def attention(x, c_attn_w, c_proj_w):
            b, t, c = x.shape
            hd = c // H
            q, k, v = jnp.split(x @ c_attn_w, 3, axis=-1)
            q = q.reshape(b, t, H, hd).transpose(0, 2, 1, 3)
            k = k.reshape(b, t, H, hd).transpose(0, 2, 1, 3)
            v = v.reshape(b, t, H, hd).transpose(0, 2, 1, 3)
            att = jnp.einsum('bhqd,bhkd->bhqk', q, k) / jnp.sqrt(jnp.asarray(hd, x.dtype))
            causal = jnp.tril(jnp.ones((t, t), bool))
            att = jnp.where(causal, att, jnp.asarray(-jnp.inf, att.dtype))
            att = jax.nn.softmax(att, axis=-1)
            y = jnp.einsum('bhqk,bhkd->bhqd', att, v)
            y = y.transpose(0, 2, 1, 3).reshape(b, t, c)
            return y @ c_proj_w

        def moe_mlp(x, router_w, w1, w2):
            b, t, c = x.shape
            xf = x.reshape(-1, c)
            router_logits = xf @ router_w
            probs = jax.nn.softmax(router_logits.astype(jnp.float32), axis=-1)
            rw, sel = jax.lax.top_k(probs, K)
            rw = rw / rw.sum(axis=-1, keepdims=True)
            rw = rw.astype(x.dtype)
            w1e = w1.reshape(c, E, F).transpose(1, 0, 2)
            w2e = w2.reshape(E, F, c)
            h = jax.nn.gelu(jnp.einsum('nc,ecf->enf', xf, w1e), approximate=False)
            y_all = jnp.einsum('enf,efc->nec', h, w2e)
            y_sel = jnp.take_along_axis(y_all, sel[:, :, None], axis=1)
            y = (y_sel * rw[:, :, None]).sum(axis=1)
            return y.reshape(b, t, c)
        x = x + attention(layernorm(x, ln1_w), c_attn_w, c_proj_w)
        x = x + moe_mlp(layernorm(x, ln2_w), router_w, w1, w2)
        return x
    x = L0_attn_x
    x = _layernorm(x + _L0_attn_ref(x, L0_attn_qkv_w, L0_attn_qkv_b, L0_attn_proj_w, L0_attn_proj_b), axis=-1)
    x = _layernorm(x + _L0_ffn_ref(x, L0_ffn_ln1_w, L0_ffn_c_attn_w, L0_ffn_c_proj_w, L0_ffn_ln2_w, L0_ffn_router_w, L0_ffn_w1, L0_ffn_w2), axis=-1)
    return x

_drawn_inputs = setup_inputs


def setup_inputs(seed=0):
    import zlib

    import numpy as np

    out = dict(_drawn_inputs(seed))
    spreads = {'L0_ffn_ln1_w': (1.0, 0.6), 'L0_ffn_ln2_w': (1.0, 0.6)}
    factors = {'L0_attn_qkv_w': 8.0,
     'L0_attn_qkv_b': 8.0,
     'L0_attn_proj_w': 8.0,
     'L0_attn_proj_b': 2.74,
     'L0_ffn_c_attn_w': 8.0,
     'L0_ffn_c_proj_w': 8.0,
     'L0_ffn_router_w': 4.765,
     'L0_ffn_w1': 4.119,
     'L0_ffn_w2': 4.066}
    for name, (base, spread) in spreads.items():
        noise = np.random.default_rng([zlib.crc32(name.encode()), seed]).standard_normal(out[name].shape)
        drawn = base * np.exp(spread * noise) if base else spread * noise
        out[name] = jnp.asarray(drawn.astype(out[name].dtype))
    for name, factor in factors.items():
        out[name] = (out[name] * factor).astype(out[name].dtype)
    return out
```

```python
import numpy as np
import concourse.bass as bass
from concourse import mybir
from contextlib import ExitStack

C = 128
SEQ, T = 32, 256
H, HD = 16, 8
E, F = 8, 256
P = 128
QUADS, J = 4, 4
PAIR = 2 * T
PAIRS = SEQ * T // PAIR
TILES = PAIR // P
NF = E * F // P
DATA = 3 * 32
ROWS = DATA + H
MSCALE = 64.0
MASKED = 60000.0
DIAG = 1024.0
EPS = 1e-5
SCALE = HD ** -0.5


class Ring:

    def __init__(self, slots, base):
        self.slots, self.base, self.used = slots, base, 0

    def next(self):
        i = self.used
        self.used += 1
        return i % self.slots, self.base + (i + 1)


class Turn:

    def __init__(self, i, off):
        self.i, self.off = i, off

    def __call__(self, per, k):
        return self.i * per + (self.off * per + k + 1)

    def raw(self, per, k):
        return self.i * per + (self.off * per + k)

    def index(self):
        return self.i + self.off if self.off else self.i


def stage_steps():

    def attention(s):
        steps = []

        def maxima(b):
            return [(s, "max", b, q) for q in range(QUADS)] + [(s, "mt", b)]

        def weights(b):
            out = []
            for u in range(8):
                out.append((s, "exp", b, u))
                if u >= 2:
                    out.append((s, "pv", b, u - 2))
                if u == 6:
                    out.append((s, "uev", b, 0))
            return out + [(s, "pv", b, 6), (s, "pv", b, 7), (s, "uev", b, 1), (s, "ut", b, 0), (s, "ut", b, 1)]

        steps += maxima(0)
        steps += merge([weights(0), maxima(1)])
        steps += weights(1)
        return steps + [(s, "ot"), (s, "proj")]

    a = [("A", "in"), ("A", "qkv"), ("A", "pack")] + attention("A") + [("A", "ln")]
    b = [("B", "ln"), ("B", "in"), ("B", "qkv"), ("B", "pack")] + attention("B")
    m = [("M", "ln"), ("M", "in"), ("M", "logits"), ("M", "route1"), ("M", "e2"), ("M", "route2")]
    m += [("M", "up", c) for c in range(NF // 2)]
    m += [("M", "down", t, g) for t in range(TILES) for g in range(2)]
    m += [("M", "out")]
    return {"A": a, "B": b, "M": m}


def merge(lists):
    keyed = []
    for n, steps in enumerate(lists):
        keyed += [((k + 0.5) / len(steps), n, k, s) for k, s in enumerate(steps)]
    return [x[3] for x in sorted(keyed, key=lambda x: x[:3])]


D_UNITS = {"A": 46, "B": 36, "M": 10}
PACKS = 16 * (3 + 3 * J)
A_UNITS = {"A": 16, "B": 16, "M": 8}


def sections():
    stages = stage_steps()
    out = []
    for lo, hi, offs in SECTIONS:
        lists = [stages[s] for s in "MBA" if s in offs]
        out.append((lo, hi, offs, interleave(lists)))
    return out


SECTIONS = [(0, PAIRS, {"A": 0, "B": 0, "M": 0})]


def interleave(lists):
    return [x for l in lists[::-1] for x in l]


def program(nc, x, w_a, b_cols, bv_row, proj_a, pb_row, ln1, w_b, proj_b, ln2, router, w1, w2,
            ident, rope, mask, ones_rows, out):
    f32, f16 = mybir.dt.float32, mybir.dt.float16
    ALU, ACT, AX = mybir.AluOpType, mybir.ActivationFunctionType, mybir.AxisListType

    x_v = x.rearrange("(n t p) c -> n p t c", t=TILES, p=P)
    out_v = out.rearrange("(n t p) c -> n p t c", t=TILES, p=P)

    ctx = ExitStack()
    with ctx:
        def sb(name, shape, dt=f32):
            return ctx.enter_context(nc.sbuf_tensor(name, shape, dt))

        def sem(name):
            return ctx.enter_context(nc.semaphore(name))

        hid = sb("hid", [P, NF, PAIR])
        wa_f = hid[:, 0:2, :].rearrange("p a n -> p (a n)")[:, 0:5 * C].rearrange("p (g c) -> p g c", g=5)
        wb_f = hid[:, 2, 0:3 * C].rearrange("p (g c) -> p g c", g=3)
        rt_f = hid[:, 3, 0:E]
        w1_f = hid[:, 4:4 + E * F // PAIR, :].rearrange("p a n -> p (a n)")
        wa = sb("wa", [P, 2, 5, C], f16)
        wb = sb("wb", [P, 2, 3, C], f16)
        w1s = sb("w1s", [P, 2, E * F], f16)
        w2s = sb("w2s", [P, NF, C])
        rts = sb("rts", [P, 2, E], f16)
        projs = {"A": sb("proj_as", [P, C]), "B": sb("proj_bs", [P, C])}
        bcol = sb("bcol", [P, 4])
        bv = sb("bv", [P, C])
        pb = sb("pb", [P, C])
        lnw = {"B": sb("ln1s", [P, 1]), "M": sb("ln2s", [P, 1])}
        idf = sb("idf", [P, P])
        big = sb("big", [P, P], f16)
        ropes = sb("ropes", [P, 2, T])
        masks = sb("masks", [P, P], f16)
        epsc = sb("epsc", [P, TILES])
        halfc = sb("halfc", [P, TILES])
        order = sb("order", [P, TILES, E])

        L = {}
        for s in "AB":
            L[s] = dict(
                xs=sb(f"xs{s}", [P, 2, PAIR], f16),
                qs=sb(f"qs{s}", [P, 2, 2, PAIR], f16),
                qp=sb(f"qp{s}", [P, QUADS, PAIR], f16),
                kz=sb(f"kz{s}", [P, QUADS, J, PAIR], f16),
                v=sb(f"v{s}", [P, TILES, H, 32]),
                mx=sb(f"mx{s}", [P, 2, 2, H]),
                mt=sb(f"mt{s}", [H, 2, T], f16),
                pt=sb(f"pt{s}", [P, 4, J, T]),
                u=sb(f"u{s}", [P, QUADS, T]),
                rec=sb(f"rec{s}", [P, 2, H]),
                o=sb(f"o{s}", [P, TILES, C]),
                scratch=nc.dram_tensor(f"scratch{s}", [2, 2, P, PAIR], f16, kind="Internal").ap(),
            )
            L[s]["ot"] = L[s]["o"][:, :, :].rearrange("p t c -> p (t c)")
        xin = sb("xin", [P, TILES, C])
        xpb = sb("xpb", [P, TILES, C])
        rot = sb("rot", [P, 4, PAIR])
        ya = sb("ya", [P, TILES, C])
        x1 = sb("x1", [P, TILES, C])
        zb = sb("zb", [P, TILES, C])
        x2 = sb("x2", [P, TILES, C])
        x12 = sb("x12", [P, TILES, C])
        zm = sb("zm", [P, TILES, C])
        xsm = sb("xsm", [P, 2, PAIR], f16)
        tmp = sb("tmp", [P, 2, 4, C])
        part = sb("part", [P, 2, C])
        half = sb("half", [P, C])
        acc = sb("acc", [P, TILES, C])
        yout = zm
        stats = {k: sb(f"stats{k}", [P, TILES, 6]) for k in ("a", "b", "m", "o")}
        mv = {k: sb(f"mv{k}", [P, TILES, 2]) for k in ("a", "b", "m", "o")}
        ve = {k: sb(f"ve{k}", [P, TILES]) for k in ("a", "b", "m", "o")}
        rstd = {k: sb(f"rstd{k}", [P, TILES]) for k in ("a", "b", "m", "o")}
        lg = sb("lg", [P, TILES, E])
        best = sb("best", [P, 2, TILES])
        eq = sb("eq", [P, TILES, E])
        turn_ = sb("turn_", [P, TILES])
        sel = sb("sel", [P, 2, TILES, E])
        rest = sb("rest", [P, TILES, E])
        diff = sb("diff", [P, TILES])
        ed = sb("ed", [P, TILES])
        den = sb("den", [P, TILES])
        wts = sb("wts", [P, 2, TILES])
        gsel = sb("gsel", [P, 2, TILES, E])
        gate = sb("gate", [P, TILES, E])

        d_ps = [ctx.enter_context(nc.psum_tensor(f"d_ps{i}", [P, 512], f32)) for i in range(2)]
        a_ps = [ctx.enter_context(nc.psum_tensor(f"a_ps{i}", [P, 1024], f32)) for i in range(2)]
        u_ps = {s: ctx.enter_context(nc.psum_tensor(f"u_ps{s}", [P, 2, T], f32)) for s in "AB"}

        loaded = sem("loaded")
        rows_set = sem("rows_set")
        wait_carried = sem("wait_carried")
        consts = sem("consts")
        zeroed = sem("zeroed")
        split_w = sem("split_w")
        d_full, d_free = sem("d_full"), sem("d_free")
        a_full, a_free = sem("a_full"), sem("a_free")
        counted = []

        def csem(name):
            counted.append(sem(name))
            return counted[-1]

        x_loaded = csem("x_loaded")
        xpb_done = csem("xpb_done")
        rot_done = csem("rot_done")
        out_stored = csem("out_stored")
        out_done = csem("out_done")
        x1_done, x2_done = csem("x1_done"), csem("x2_done")
        S = {}
        for s in "AB":
            S[s] = {k: csem(f"{k}_{s}") for k in (
                "xs_done",
                "split_done",
                "stored",
                "packed",
                "v_done",
                "mx_done",
                "mt_done",
                "exp_done",
                "pv_done",
                "u_done",
                "o_done",
                "ot_done",
            )}
            S[s]["mrows"] = [csem(f"mrows{b}_{s}") for b in range(2)]
        x12_done = csem("x12_done")
        masked = csem("masked")
        z_done = {s: csem(f"z_done{s}") for s in "BM"}
        stats_done = {k: csem(f"stats_done_{k}") for k in ("a", "b", "m", "o")}
        rstd_done = {k: csem(f"rstd_done_{k}") for k in ("a", "b", "m", "o")}
        xsm_done = csem("xsm_done")
        diff_done, ed_done, gate_done = csem("diff_done"), csem("ed_done"), csem("gate_done")
        hid_done = csem("hid_done")
        gated = csem("gated")
        summed = csem("summed")
        dve_link = {s: sem(f"dve_link_{s}") for s in "ABM"}
        pool_link = {s: sem(f"pool_link_{s}") for s in "ABM"}
        DVE_LINKS = {"A": 7, "B": 9, "M": 19}
        POOL_LINKS = {"A": 5, "B": 1, "M": 18}

        N_LOADS = 15
        plan = sections()

        class Now:

            def __init__(self, i, lo, offs, base, links=None):
                self.turn = {s: Turn(i, o) for s, o in offs.items()}
                nd = sum(D_UNITS[s] for s in offs)
                na = sum(A_UNITS[s] for s in offs)
                if isinstance(i, int):
                    self.d, self.a = Ring(2, base[0]), Ring(2, base[1])
                else:
                    self.d, self.a = Ring(2, i * nd + (base[0] - lo * nd)), Ring(2, i * na + (base[1] - lo * na))
                self.per, self.k = links, {s: 0 for s in offs}

            def link(self, s):
                self.k[s] += 1
                return self.turn[s].raw(self.per[s], self.k[s])

            def end(self):
                for s, k in self.k.items():
                    assert self.per is None or k == self.per[s], (s, k, self.per[s])

        def walk(eng, do, links=None):
            base = [0, 0]
            for lo, hi, offs, steps in plan:
                def turn(i):
                    now = Now(i, lo, offs, tuple(base), links)
                    for step in steps:
                        do(now, *step)
                    now.end()
                if hi - lo == 1:
                    turn(lo)
                else:
                    with eng.Fori(lo, hi) as i:
                        turn(i)
                base[0] += (hi - lo) * sum(D_UNITS[s] for s in offs)
                base[1] += (hi - lo) * sum(A_UNITS[s] for s in offs)

        block = ctx.enter_context(nc.Block())

        @block.sync
        def _(sp):
            for dst, src in ((wa_f, w_a), (bcol[:, :], b_cols), (wb_f, w_b),
                             (idf[:, :], ident), (ropes[:, :, :], rope), (bv[:, :], bv_row.partition_broadcast(P)),
                             (pb[:, :], pb_row.partition_broadcast(P)), (projs["A"][:, :], proj_a),
                             (masks[:, :], mask), (lnw["B"][:, :], ln1), (projs["B"][:, :], proj_b),
                             (lnw["M"][:, :], ln2), (rt_f, router), (w1_f, w1),
                             (w2s[:, :, :], w2)):
                sp.dma_start(dst, src).then_inc(loaded, 16)
            sp.wait_ge(zeroed, 2)
            for s in "AB":
                sp.dma_start(L[s]["kz"][DATA:ROWS, :, :, :], ones_rows).then_inc(rows_set, 16)

            def do(now, s, step, *args):
                t = now.turn[s]
                if (s, step) == ("A", "in"):
                    sp.wait_ge(S["A"]["xs_done"], t(1, 0))
                    sp.wait_ge(xpb_done, t(1, 0))
                    sp.dma_start(xin[:, :, :], x_v[t.index(), :, :, :]).then_inc(x_loaded, 16)
                if step == "pack":
                    B, Z = L[s], S[s]
                    sp.wait_ge(Z["packed"], t(PACKS, 0))
                    for w in range(2):
                        sp.wait_ge(Z["split_done"], t(2, w + 1))
                        sp.dma_start(B["scratch"][w].rearrange("h p n -> p h n"), B["qs"][:, w, :, :]).then_inc(Z["stored"], 16)
                    sp.wait_ge(Z["pv_done"], t(16, 3))
                    sp.wait_ge(Z["stored"], t(32, 32))
                    q_src, k_src = B["scratch"][0], B["scratch"][1]
                    for c, h in ((0, 0), (1, 0), (2, 1)):
                        sp.dma_start(B["qp"][32 * c:32 * c + 32, :, :],
                                     q_src[h].rearrange("(q r) n -> r q n", q=QUADS)).then_inc(Z["packed"], 16)
                    for c, h in ((0, 0), (1, 1), (2, 0)):
                        for j in range(J):
                            r = 32 * c + HD * j
                            sp.dma_start(B["kz"][r:r + HD, :, j, :],
                                         k_src[h].rearrange("(q j d) n -> j d q n", q=QUADS, j=J)[j]).then_inc(Z["packed"], 16)
                if step == "mt":
                    b, = args
                    sp.wait_ge(S[s]["mt_done"], t(2, b + 1))
                    for q in range(QUADS):
                        sp.dma_start(L[s]["qp"][DATA:ROWS, q, b * T:(b + 1) * T], L[s]["mt"][:, b, :]).then_inc(S[s]["mrows"][b], 16)
                if step == "out":
                    sp.wait_ge(out_done, t(1, 1))
                    sp.dma_start(out_v[t.index(), :, :, :], yout[:, :, :]).then_inc(out_stored, 16)

            for q in counted[0::4]:
                sp.sem_inc(q, 1)
            walk(sp, do)
            sp.wait_ge(out_stored, 1 + 16 * PAIRS)

        @block.gpsimd
        def _(pool):
            for q in counted[1::4]:
                pool.sem_inc(q, 1)
            pool.sem_inc(summed, 1)
            for s in "AB":
                pool.sem_inc(S[s]["pv_done"], 3)
            pool.memset(epsc[:, :], EPS).then_inc(consts, 1)
            pool.memset(halfc[:, :], -0.5).then_inc(consts, 1)
            for e in range(E):
                pool.memset(order[:, :, e:e + 1], float(E - e))
            pool.memset(L["A"]["v"][:, :, :, :], 0.0).then_inc(consts, 1)
            pool.memset(L["B"]["v"][:, :, :, :], 0.0).then_inc(consts, 1)
            pool.wait_ge(consts, 4)
            for s in "AB":
                pool.memset(L[s]["v"][:, :, :, HD:HD + 1], 1.0).then_inc(consts, 1)
            pool.wait_ge(loaded, 16 * N_LOADS)
            pool.tensor_scalar(big[:, :], idf[:, :], DIAG, 0.0, ALU.mult, ALU.add).then_inc(consts, 1)

            def do(now, s, step, *args):
                t = now.turn[s]

                def rsqrt(k, per_pair_credit=True):
                    pool.wait_ge(stats_done[k], t(1, 1))
                    pool.tensor_tensor(ve[k][:, :], mv[k][:, :, 1], epsc[:, :], ALU.add).then_inc(pool_link[s], 1)
                    pool.wait_ge(pool_link[s], now.link(s))
                    pool.tensor_tensor(rstd[k][:, :], ve[k][:, :], halfc[:, :], ALU.pow).then_inc(rstd_done[k], 1)

                if (s, step) == ("A", "in"):
                    pool.wait_ge(x_loaded, t(16, 16))
                    pool.wait_ge(x1_done, t(1, 0))
                    pool.tensor_tensor(xpb[:, :, :], xin[:, :, :], pb[:, :].unsqueeze(1).to_broadcast([P, TILES, C]), ALU.add).then_inc(xpb_done, 1)
                if (s, step) == ("A", "qkv"):
                    for w in range(2):
                        pool.wait_ge(rot_done, t(4, 2 * w + 2))
                        pool.wait_ge(S["A"]["stored"], t(32, 0))
                        pool.tensor_tensor(L["A"]["qs"][:, w, 0, :], rot[:, 2 * w, :], rot[:, 2 * w + 1, :], ALU.add).then_inc(pool_link["A"], 1)
                        pool.wait_ge(pool_link["A"], now.link("A"))
                        pool.tensor_tensor(rot[:, 2 * w, :], rot[:, 2 * w, :], rot[:, 2 * w + 1, :], ALU.add).then_inc(pool_link["A"], 1)
                        pool.wait_ge(pool_link["A"], now.link("A"))
                        pool.tensor_tensor(L["A"]["qs"][:, w, 1, :], rot[:, 2 * w, :], L["A"]["qs"][:, w, 0, :], ALU.subtract).then_inc(S["A"]["split_done"], 1)
                if (s, step) == ("A", "ln"):
                    rsqrt("a")
                if (s, step) == ("B", "ln"):
                    rsqrt("b")
                if (s, step) == ("M", "ln"):
                    rsqrt("m")
                if (s, step) == ("M", "out"):
                    rsqrt("o")
                if (s, step) == ("B", "proj"):
                    pool.wait_ge(x2_done, t(1, 1))
                    pool.tensor_tensor(x12[:, :, :], x2[:, :, :], x1[:, :, :], ALU.add).then_inc(x12_done, 1)
                if (s, step) == ("B", "exp"):
                    b, u = args
                    kt = u % 2
                    pool.wait_ge(S["B"]["exp_done"], t(16, 8 * b + u + 1))
                    pool.sem_inc(wait_carried, 1)
                    v = L["B"]["pt"][:, u % 4, :, kt * P:(kt + 1) * P]
                    pool.affine_select(out=v, in_=v, pattern=[[0, J], [1, P]], compare_op=ALU.is_ge, fill=0.0,
                                       base=0, channel_multiplier=-1).then_inc(masked, 1)
                if (s, step) == ("M", "down"):
                    tile, g = args
                    n = 2 * tile + g
                    pool.wait_ge(gated, t(8, n + 1))
                    if n == 0:
                        pool.wait_ge(out_done, t(1, 0))
                        pool.wait_ge(x12_done, t(1, 1))
                    tm = tmp[:, n % 2]
                    pool.tensor_tensor(part[:, :, :], tm[:, 0:2, :], tm[:, 2:4, :], ALU.add).then_inc(pool_link["M"], 1)
                    pool.wait_ge(pool_link["M"], now.link("M"))
                    pool.tensor_tensor(half[:, :], part[:, 0, :], part[:, 1, :], ALU.add).then_inc(pool_link["M"], 1)
                    pool.wait_ge(pool_link["M"], now.link("M"))
                    pool.tensor_tensor(acc[:, tile, :], half[:, :], x12[:, tile, :] if g == 0 else acc[:, tile, :], ALU.add).then_inc(summed, 1)
                    pool.wait_ge(summed, t(8, n + 2))

            walk(pool, do, {"A": POOL_LINKS["A"], "B": POOL_LINKS["B"], "M": POOL_LINKS["M"]})

        @block.scalar
        def _(act):
            for q in counted[2::4]:
                act.sem_inc(q, 1)
            act.sem_inc(a_free, 2)

            def do(now, s, step, *args):
                t = now.turn[s]
                if step == "exp":
                    b, u = args
                    B, Z = L[s], S[s]
                    slot, count = now.a.next()
                    n = 8 * b + u
                    act.wait_ge(a_full, count)
                    act.wait_ge(Z["pv_done"], t(16, n))
                    if s == "B" and u % 2:
                        dst, src = B["pt"][:, u % 4, :, P:T], a_ps[slot][:, 0:J * P].rearrange("p (j n) -> p j n", j=J)
                    else:
                        dst, src = B["pt"][:, u % 4, :, :], a_ps[slot][:, :].rearrange("p (j n) -> p j n", j=J)
                    act.activation(dst, src, ACT.Exp, scale=SCALE).then_inc(Z["exp_done"], 1)
                    act.wait_ge(Z["exp_done"], t(16, n + 1))
                    act.sem_inc(a_free, 1)
                if step == "uev":
                    b, half_ = args
                    B, Z = L[s], S[s]
                    act.wait_ge(Z["pv_done"], t(16, 8 * b + 4 * half_ + 4 + 3))
                    act.wait_ge(Z["o_done"], t(4, 2 * b))
                    act.activation(B["u"][:, 2 * half_:2 * half_ + 2, :], u_ps[s][:, :, :], ACT.Copy).then_inc(Z["u_done"], 1)
                if step == "e2":
                    act.wait_ge(diff_done, t(1, 1))
                    act.wait_ge(gate_done, t(1, 0))
                    act.activation(ed[:, :], diff[:, :], ACT.Exp).then_inc(ed_done, 1)
                if step == "up":
                    c, = args
                    slot, count = now.a.next()
                    act.wait_ge(a_full, count)
                    if c == 0:
                        act.wait_ge(gated, t(8, 0))
                    act.activation(hid[:, 2 * c:2 * c + 2, :], a_ps[slot][:, :].rearrange("p (c n) -> p c n", c=2), ACT.Gelu).then_inc(hid_done, 1)
                    act.wait_ge(hid_done, t(8, c + 1))
                    act.sem_inc(a_free, 1)

            walk(act, do)

        @block.tensor
        def _(pe):
            for q in counted[3::4]:
                pe.sem_inc(q, 1)
            pe.wait_ge(loaded, 16 * N_LOADS)
            pe.wait_ge(rows_set, 32)
            pe.wait_ge(consts, 7)
            pe.wait_ge(split_w, 8)

            def three(dst, wide, moving):
                for n, (a, b) in enumerate(((0, 0), (1, 0), (0, 1))):
                    last = pe.matmul(dst, wide(a), moving(b), start=n == 0, stop=n == 2)
                return last

            def turned(now, src):
                slot, count = now.d.next()
                pe.wait_ge(d_free, count)
                for i in range(TILES):
                    last = pe.transpose(d_ps[slot][:, i * P:(i + 1) * P], src[:, i, :], idf[:, :])
                last.then_inc(d_full, 1)

            def do(now, s, step, *args):
                t = now.turn[s]
                if step == "in":
                    if s == "A":
                        pe.wait_ge(x_loaded, t(16, 16))
                        turned(now, xin)
                    else:
                        pe.wait_ge(z_done[s], t(1, 1))
                        turned(now, zb if s == "B" else zm)
                if step == "qkv":
                    xs, w = L[s]["xs"], wa if s == "A" else wb
                    pe.wait_ge(S[s]["xs_done"], t(1, 1))
                    n_t = 4 if s == "A" else 2
                    for g in range(n_t):
                        slot, count = now.d.next()
                        pe.wait_ge(d_free, count)
                        three(d_ps[slot][:, :], lambda a: w[:, a, g, :], lambda b: xs[:, b, :]).then_inc(d_full, 1)
                    slot, count = now.d.next()
                    pe.wait_ge(d_free, count)
                    for i in range(TILES):
                        last = three(d_ps[slot][:, i * P:(i + 1) * P], lambda a: xs[:, a, i * P:(i + 1) * P],
                                     lambda b: w[:, b, n_t, :])
                    last.then_inc(d_full, 1)
                if step == "max":
                    b, q = args
                    B = L[s]
                    if b == 0 and q == 0:
                        pe.wait_ge(S[s]["packed"], t(PACKS, PACKS))
                    for qt in range(2):
                        at = b * T + qt * P
                        wide = B["qp"][0:DATA, q, at:at + P]
                        if s == "B" and qt == 0:
                            slot, count = now.d.next()
                            pe.wait_ge(d_free, count)
                            pe.matmul(d_ps[slot][:, :], wide, B["kz"][0:DATA, q, :, b * T:b * T + P], start=True, stop=False)
                            pe.matmul(d_ps[slot][:, :], big[:, :], masks[:, :].unsqueeze(1).to_broadcast([P, J, P]),
                                      start=False, stop=True).then_inc(d_full, 1)
                            continue
                        for h in range(2):
                            slot, count = now.d.next()
                            pe.wait_ge(d_free, count)
                            last = pe.matmul(d_ps[slot][:, :], wide, B["kz"][0:DATA, q, 2 * h:2 * h + 2, b * T:(b + 1) * T],
                                             start=True, stop=s == "A")
                            if s == "B":
                                last = pe.matmul(d_ps[slot][:, :].rearrange("p (j n) -> p j n", j=2)[:, :, P:T], big[:, :],
                                                 masks[:, :].unsqueeze(1).to_broadcast([P, 2, P]), start=False, stop=True)
                            last.then_inc(d_full, 1)
                if step == "mt":
                    b, = args
                    pe.wait_ge(S[s]["mx_done"], t(2, b + 1))
                    slot, count = now.d.next()
                    pe.wait_ge(d_free, count)
                    for qt in range(2):
                        last = pe.transpose(d_ps[slot][0:H, qt * P:(qt + 1) * P], L[s]["mx"][:, b, qt, :], idf[:, :])
                    last.then_inc(d_full, 1)
                if step == "exp":
                    b, u = args
                    B = L[s]
                    q, kt = u // 2, u % 2
                    if u == 0:
                        pe.wait_ge(S[s]["mrows"][b], t(64, 64))
                    slot, count = now.a.next()
                    pe.wait_ge(a_free, count)
                    first = P if s == "B" and kt else 0
                    n = T - first
                    for j in range(J):
                        last = pe.matmul(a_ps[slot][:, j * n:(j + 1) * n], B["kz"][0:ROWS, q, j, b * T + kt * P:b * T + (kt + 1) * P],
                                         B["qp"][0:ROWS, q, b * T + first:(b + 1) * T], start=True, stop=True)
                    last.then_inc(a_full, 1)
                if step == "pv":
                    b, u = args
                    B, Z = L[s], S[s]
                    q, kt = u // 2, u % 2
                    if b == 0 and u == 0:
                        pe.wait_ge(Z["v_done"], t(1, 1))
                    pe.wait_ge(masked if s == "B" else Z["exp_done"], t(16, 8 * b + u + 1))
                    if u % 4 == 0:
                        pe.wait_ge(Z["u_done"], t(4, 2 * b + u // 4))
                    first = P if s == "B" and kt else 0
                    for j in range(J):
                        last = pe.matmul(u_ps[s][32 * j:32 * j + 32, q % 2, first:T], B["v"][:, 2 * b + kt, J * q + j, :],
                                         B["pt"][:, u % 4, j, first:T], start=kt == 0, stop=kt == 1)
                    last.then_inc(Z["pv_done"], 1)
                if step == "ut":
                    b, qt = args
                    pe.wait_ge(S[s]["u_done"], t(4, 2 * b + 2))
                    slot, count = now.d.next()
                    pe.wait_ge(d_free, count)
                    for q in range(QUADS):
                        last = pe.transpose(d_ps[slot][:, q * P:(q + 1) * P], L[s]["u"][:, q, qt * P:(qt + 1) * P], idf[:, :])
                    last.then_inc(d_full, 1)
                if step == "ot":
                    pe.wait_ge(S[s]["o_done"], t(4, 4))
                    turned(now, L[s]["o"])
                if step == "proj":
                    pe.wait_ge(S[s]["ot_done"], t(1, 1))
                    slot, count = now.d.next()
                    pe.wait_ge(d_free, count)
                    for i in range(TILES):
                        last = pe.matmul(d_ps[slot][:, i * P:(i + 1) * P], L[s]["ot"][:, i * P:(i + 1) * P], projs[s][:, :],
                                         start=True, stop=True)
                    last.then_inc(d_full, 1)
                if step == "logits":
                    pe.wait_ge(xsm_done, t(1, 1))
                    slot, count = now.d.next()
                    pe.wait_ge(d_free, count)
                    for i in range(TILES):
                        last = three(d_ps[slot][:, i * E:(i + 1) * E], lambda a: xsm[:, a, i * P:(i + 1) * P], lambda b: rts[:, b, :])
                    last.then_inc(d_full, 1)
                if step == "up":
                    c, = args
                    slot, count = now.a.next()
                    pe.wait_ge(a_free, count)
                    for k in range(2):
                        f = 2 * c + k
                        last = three(a_ps[slot][:, k * PAIR:(k + 1) * PAIR], lambda a: w1s[:, a, f * P:(f + 1) * P], lambda b: xsm[:, b, :])
                    last.then_inc(a_full, 1)
                if step == "down":
                    tile, g = args
                    if g == 0:
                        pe.wait_ge(hid_done, t(8, 8))
                    slot, count = now.d.next()
                    pe.wait_ge(d_free, count)
                    for e in range(4):
                        for k in range(2):
                            f = 2 * (4 * g + e) + k
                            last = pe.matmul(d_ps[slot][:, e * C:(e + 1) * C], hid[:, f, tile * P:(tile + 1) * P], w2s[:, f, :],
                                             start=k == 0, stop=k == 1)
                    last.then_inc(d_full, 1)

            walk(pe, do)

        @block.vector
        def _(dve):
            dve.sem_inc(d_free, 2)
            for s in "AB":
                dve.memset(L[s]["kz"][:, :, :, :], 0.0).then_inc(zeroed, 1)
            dve.wait_ge(loaded, 16 * N_LOADS)
            k = 0
            for f, hl in ((wa_f, lambda h: wa[:, h, :, :]), (wb_f, lambda h: wb[:, h, :, :]),
                          (w1_f, lambda h: w1s[:, h, :]), (rt_f, lambda h: rts[:, h, :])):
                dve.tensor_copy(hl(0), f).then_inc(split_w, 1)
                k += 1
                dve.wait_ge(split_w, k)
                dve.tensor_tensor(hl(1), f, hl(0), ALU.subtract).then_inc(split_w, 1)
                k += 1
            dve.wait_ge(consts, 7)

            def ring(now):
                slot, count = now.d.next()
                dve.wait_ge(d_full, count)
                return d_ps[slot]

            def do(now, s, step, *args):
                t = now.turn[s]
                link = dve_link[s]

                def stats_of(k, src):
                    for i in range(TILES):
                        last = dve.bn_stats(stats[k][:, i, :], src[:, i, :])
                    last.then_inc(link, 1)
                    dve.wait_ge(link, now.link(s))
                    dve.sem_inc(wait_carried, 1)
                    for i in range(TILES):
                        last = dve.bn_aggr(mv[k][:, i, :], stats[k][:, i, :])
                    last.then_inc(stats_done[k], 1)

                def normalised(k, dst, src, done):
                    dve.wait_ge(rstd_done[k], t(1, 1))
                    for i in range(TILES):
                        last = dve.tensor_scalar(dst[:, i, :], src[:, i, :], mv[k][:, i, 0:1], rstd[k][:, i:i + 1], ALU.subtract, ALU.mult)
                    last.then_inc(done, 1)

                if step == "in":
                    xs = xsm if s == "M" else L[s]["xs"]
                    if s == "M":
                        dve.wait_ge(hid_done, t(8, 0))
                    ps = ring(now)
                    if s == "A":
                        dve.tensor_copy(xs[:, 0, :], ps[:, :]).then_inc(link, 1)
                        dve.wait_ge(link, now.link(s))
                        dve.tensor_tensor(xs[:, 1, :], ps[:, :], xs[:, 0, :], ALU.subtract).then_inc(S["A"]["xs_done"], 1)
                        dve.wait_ge(S["A"]["xs_done"], t(1, 1))
                    else:
                        dve.tensor_scalar(xs[:, 0, :], ps[:, :], lnw[s][:, 0:1], None, ALU.mult).then_inc(link, 1)
                        dve.wait_ge(link, now.link(s))
                        done = xsm_done if s == "M" else S[s]["xs_done"]
                        dve.scalar_tensor_tensor(xs[:, 1, :], ps[:, :], lnw[s][:, 0:1], xs[:, 0, :], ALU.mult, ALU.subtract).then_inc(done, 1)
                        dve.wait_ge(done, t(1, 1))
                    dve.sem_inc(d_free, 1)
                if (s, step) == ("A", "qkv"):
                    dve.wait_ge(S["A"]["split_done"], t(2, 0))
                    for g in range(4):
                        ps = ring(now)
                        dve.scalar_tensor_tensor(rot[:, g, :].rearrange("p (b n) -> p b n", b=2), ps[:, :].rearrange("p (b n) -> p b n", b=2),
                                                 bcol[:, g:g + 1], ropes[:, g % 2, :].unsqueeze(1).to_broadcast([P, 2, T]),
                                                 ALU.add, ALU.mult).then_inc(rot_done, 1)
                        dve.wait_ge(rot_done, t(4, g + 1))
                        dve.sem_inc(d_free, 1)
                if (s, step) == ("B", "qkv"):
                    dve.wait_ge(S["B"]["stored"], t(32, 0))
                    for g in range(2):
                        ps = ring(now)
                        qs = L["B"]["qs"]
                        dve.tensor_copy(qs[:, g, 0, :], ps[:, :]).then_inc(link, 1)
                        dve.wait_ge(link, now.link(s))
                        dve.tensor_tensor(qs[:, g, 1, :], ps[:, :], qs[:, g, 0, :], ALU.subtract).then_inc(S["B"]["split_done"], 1)
                        dve.wait_ge(S["B"]["split_done"], t(2, g + 1))
                        dve.sem_inc(d_free, 1)
                if step == "qkv":
                    dve.wait_ge(S[s]["pv_done"], t(16, 3))
                    ps = ring(now)
                    v = L[s]["v"]
                    for i in range(TILES):
                        src = ps[:, i * P:(i + 1) * P].rearrange("p (h d) -> p h d", d=HD)
                        if s == "A":
                            last = dve.tensor_tensor(v[:, i, :, 0:HD], src, bv[:, :].rearrange("p (h d) -> p h d", d=HD), ALU.add)
                        else:
                            last = dve.tensor_copy(v[:, i, :, 0:HD], src)
                    last.then_inc(S[s]["v_done"], 1)
                    dve.wait_ge(S[s]["v_done"], t(1, 1))
                    dve.sem_inc(d_free, 1)
                if step == "max":
                    b, q = args
                    mx = L[s]["mx"]
                    for qt in range(2):
                        if s == "B" and qt == 0:
                            ps = ring(now)
                            dve.tensor_reduce(mx[:, b, 0, J * q:J * q + J], ps[:, :].rearrange("p (j n) -> p j n", j=J), AX.X, ALU.max).then_inc(d_free, 1)
                            continue
                        for h in range(2):
                            ps = ring(now)
                            at = J * q + 2 * h
                            dve.tensor_reduce(mx[:, b, qt, at:at + 2], ps[:, :].rearrange("p (j n) -> p j n", j=2), AX.X, ALU.max).then_inc(d_free, 1)
                    if q == QUADS - 1:
                        dve.wait_ge(d_free, now.d.base + (now.d.used + 2))
                        dve.sem_inc(S[s]["mx_done"], 1)
                if step == "mt":
                    b, = args
                    for bb in range(2):
                        dve.wait_ge(S[s]["mrows"][bb], t(64, 0))
                    ps = ring(now)
                    dve.tensor_scalar(L[s]["mt"][:, b, :], ps[0:H, 0:T], -1.0 / MSCALE, None, ALU.mult).then_inc(S[s]["mt_done"], 1)
                    dve.wait_ge(S[s]["mt_done"], t(2, b + 1))
                    dve.sem_inc(d_free, 1)
                if step == "ut":
                    b, qt = args
                    B = L[s]
                    ps = ring(now)
                    v = ps[:, :].rearrange("p (h r) -> p h r", r=32)
                    dve.reciprocal(B["rec"][:, qt, :], v[:, :, HD]).then_inc(link, 1)
                    dve.wait_ge(link, now.link(s))
                    dve.tensor_tensor(B["o"][:, 2 * b + qt, :].rearrange("p (h d) -> p h d", d=HD), v[:, :, 0:HD],
                                      B["rec"][:, qt, :].unsqueeze(2).to_broadcast([P, H, HD]), ALU.mult).then_inc(S[s]["o_done"], 1)
                    dve.wait_ge(S[s]["o_done"], t(4, 2 * b + qt + 1))
                    dve.sem_inc(d_free, 1)
                if step == "ot":
                    ps = ring(now)
                    dve.tensor_copy(L[s]["ot"], ps[:, :]).then_inc(S[s]["ot_done"], 1)
                    dve.wait_ge(S[s]["ot_done"], t(1, 1))
                    dve.sem_inc(d_free, 1)
                if step == "proj":
                    if s == "A":
                        dve.wait_ge(xpb_done, t(1, 1))
                        dst, res = ya, xpb
                    else:
                        dve.wait_ge(x12_done, t(1, 0))
                        dst, res = x2, x1
                    ps = ring(now)
                    dve.tensor_tensor(dst[:, :, :], ps[:, :].rearrange("p (t c) -> p t c", t=TILES), res[:, :, :], ALU.add).then_inc(link, 1)
                    dve.wait_ge(link, now.link(s))
                    dve.sem_inc(d_free, 1)
                    if s == "B":
                        dve.sem_inc(x2_done, 1)
                if (s, step) == ("A", "ln"):
                    stats_of("a", ya)
                    dve.wait_ge(x12_done, t(1, 0))
                    normalised("a", x1, ya, x1_done)
                    dve.wait_ge(x1_done, t(1, 1))
                if (s, step) == ("B", "ln"):
                    stats_of("b", x1)
                    normalised("b", zb, x1, z_done["B"])
                if (s, step) == ("M", "ln"):
                    stats_of("m", x2)
                    dve.wait_ge(out_stored, t(16, 0))
                    normalised("m", zm, x2, z_done["M"])
                if step == "logits":
                    ps = ring(now)
                    dve.tensor_copy(lg[:, :, :], ps[:, 0:TILES * E].rearrange("p (t e) -> p t e", e=E)).then_inc(link, 1)
                    dve.wait_ge(link, now.link(s))
                    dve.sem_inc(d_free, 1)

                def wide(ap):
                    return ap.unsqueeze(2).to_broadcast([P, TILES, E])

                def choose(n, src):
                    dve.tensor_reduce(best[:, n, :], src, AX.X, ALU.max).then_inc(link, 1)
                    dve.wait_ge(link, now.link(s))
                    dve.tensor_tensor(eq[:, :, :], src, wide(best[:, n, :]), ALU.is_ge).then_inc(link, 1)
                    dve.wait_ge(link, now.link(s))
                    dve.tensor_tensor(eq[:, :, :], eq[:, :, :], order[:, :, :], ALU.mult).then_inc(link, 1)
                    dve.wait_ge(link, now.link(s))
                    dve.tensor_reduce(turn_[:, :], eq[:, :, :], AX.X, ALU.max).then_inc(link, 1)
                    dve.wait_ge(link, now.link(s))
                    dve.tensor_tensor(sel[:, n, :, :], eq[:, :, :], wide(turn_[:, :]), ALU.is_equal).then_inc(link, 1)
                    dve.wait_ge(link, now.link(s))

                if step == "route1":
                    choose(0, lg[:, :, :])
                    dve.scalar_tensor_tensor(rest[:, :, :], sel[:, 0, :, :], -3.0e38, lg[:, :, :], ALU.mult, ALU.add).then_inc(link, 1)
                    dve.wait_ge(link, now.link(s))
                    choose(1, rest[:, :, :])
                    dve.tensor_tensor(diff[:, :], best[:, 1, :], best[:, 0, :], ALU.subtract).then_inc(diff_done, 1)
                if step == "route2":
                    dve.wait_ge(ed_done, t(1, 1))
                    dve.tensor_scalar(den[:, :], ed[:, :], 1.0, None, ALU.add).then_inc(link, 1)
                    dve.wait_ge(link, now.link(s))
                    dve.reciprocal(wts[:, 0, :], den[:, :]).then_inc(link, 1)
                    dve.wait_ge(link, now.link(s))
                    dve.tensor_tensor(wts[:, 1, :], wts[:, 0, :], ed[:, :], ALU.mult).then_inc(link, 1)
                    dve.wait_ge(link, now.link(s))
                    for n in range(2):
                        last = dve.tensor_tensor(gsel[:, n, :, :], sel[:, n, :, :], wide(wts[:, n, :]), ALU.mult)
                    last.then_inc(link, 1)
                    dve.wait_ge(link, now.link(s))
                    dve.tensor_tensor(gate[:, :, :], gsel[:, 0, :, :], gsel[:, 1, :, :], ALU.add).then_inc(gate_done, 1)
                    dve.wait_ge(gate_done, t(1, 1))
                if step == "down":
                    tile, g = args
                    n = 2 * tile + g
                    dve.wait_ge(summed, t(8, n))
                    ps = ring(now)
                    dve.tensor_tensor(tmp[:, n % 2], ps[:, :].rearrange("p (e c) -> p e c", e=4),
                                      gate[:, tile, 4 * g:4 * g + 4].unsqueeze(2).to_broadcast([P, 4, C]), ALU.mult).then_inc(gated, 1)
                    dve.wait_ge(gated, t(8, n + 1))
                    dve.sem_inc(d_free, 1)
                if (s, step) == ("M", "out"):
                    dve.wait_ge(summed, t(8, 8 + 1))
                    stats_of("o", acc)
                    normalised("o", yout, acc, out_done)

            walk(dve, do, DVE_LINKS)


_INS = ["x", "w_a", "b_cols", "bv_row", "proj_a", "pb_row", "ln1", "w_b", "proj_b", "ln2", "router", "w1", "w2",
        "ident", "rope", "mask", "ones_rows"]


def constants():
    pos = np.arange(T, dtype=np.float32)
    inv = (1.0 / np.float32(10000.0) ** (np.arange(0, HD, 2, dtype=np.float32) / np.float32(HD))).astype(np.float32)
    freqs = pos[None, :] * inv[:, None]
    cos, sin = np.cos(freqs), np.sin(freqs)
    d = np.arange(P) % HD
    sign = np.where(d % 2 == 0, -1.0, 1.0)[:, None].astype(np.float32)
    rope = np.stack([cos[d // 2], sin[d // 2] * sign], axis=1).astype(np.float32)
    q, k = np.arange(P)[:, None], np.arange(P)[None, :]
    mask = np.where(k > q, -MASKED, 0.0).astype(np.float16)
    rows = np.zeros((H, QUADS, J, PAIR), np.float16)
    for h in range(H):
        rows[h, h // J, h % J, :] = MSCALE
    return {"ident": np.eye(P, dtype=np.float32), "rope": rope, "mask": mask, "ones_rows": rows}


def kernel(L0_attn_x, L0_attn_qkv_w, L0_attn_qkv_b, L0_attn_proj_w, L0_attn_proj_b, L0_ffn_ln1_w,
           L0_ffn_c_attn_w, L0_ffn_c_proj_w, L0_ffn_ln2_w, L0_ffn_router_w, L0_ffn_w1, L0_ffn_w2):
    import concourse.bacc as bacc
    from concourse.bass_utils import run_bass_kernel_spmd

    swapped = np.arange(C) ^ 1
    w = np.asarray(L0_attn_qkv_w).reshape(3, C, C)
    bias = np.asarray(L0_attn_qkv_b).reshape(3, C)
    arrays = {
        "x": np.asarray(L0_attn_x).reshape(SEQ * T, C),
        "w_a": np.stack([w[0].T, w[0][swapped].T, w[1].T, w[1][swapped].T, w[2].T], axis=1),
        "b_cols": np.stack([bias[0], bias[0][swapped], bias[1], bias[1][swapped]], axis=1),
        "bv_row": bias[2],
        "proj_a": np.asarray(L0_attn_proj_w).T,
        "pb_row": np.asarray(L0_attn_proj_b),
        "ln1": np.asarray(L0_ffn_ln1_w).reshape(C, 1),
        "w_b": np.asarray(L0_ffn_c_attn_w).reshape(C, 3, C),
        "proj_b": np.asarray(L0_ffn_c_proj_w),
        "ln2": np.asarray(L0_ffn_ln2_w).reshape(C, 1),
        "router": np.asarray(L0_ffn_router_w),
        "w1": np.asarray(L0_ffn_w1),
        "w2": np.asarray(L0_ffn_w2).reshape(NF, P, C).transpose(1, 0, 2),
        **constants(),
    }
    arrays = {k: np.ascontiguousarray(v) for k, v in arrays.items()}
    nc = bacc.Bacc("TRN2", target_bir_lowering=False, num_devices=1)
    args = [nc.dram_tensor(f"in_{k}", arrays[k].shape, mybir.dt.from_np(arrays[k].dtype), kind="ExternalInput").ap() for k in _INS]
    out = nc.dram_tensor("out_0", (SEQ * T, C), mybir.dt.float32, kind="ExternalOutput").ap()
    program(nc, *args, out)
    r = run_bass_kernel_spmd(nc, [{f"in_{k}": arrays[k] for k in _INS}], core_ids=[0])
    return r.results[0]["out_0"].reshape(SEQ, T, C)
```

```python
import numpy as np
import concourse.bass as bass
from concourse import mybir
from contextlib import ExitStack

C = 128
SEQ, T = 32, 256
H, HD = 16, 8
E, F = 8, 256
P = 128
QUADS, J = 4, 4
PAIR = 2 * T
PAIRS = SEQ * T // PAIR
TILES = PAIR // P
NF = E * F // P
DATA = 3 * 32
ROWS = DATA + H
MSCALE = 64.0
MASKED = 60000.0
DIAG = 1024.0
EPS = 1e-5
SCALE = HD ** -0.5


class Ring:

    def __init__(self, slots, base):
        self.slots, self.base, self.used = slots, base, 0

    def next(self):
        i = self.used
        self.used += 1
        return i % self.slots, self.base + (i + 1)

    def freed(self, i):
        return self.base + (i + 3)


class Turn:

    def __init__(self, i, off):
        self.i, self.off = i, off

    def __call__(self, per, k):
        return self.i * per + (self.off * per + k + 1)

    def raw(self, per, k):
        return self.i * per + (self.off * per + k)

    def index(self):
        return self.i + self.off if self.off else self.i


def merge(*lists):
    keyed = []
    for n, steps in enumerate(lists):
        keyed += [((k + 0.5) / len(steps), n, k, s) for k, s in enumerate(steps)]
    return [x[3] for x in sorted(keyed, key=lambda x: x[:3])]


def turn_steps():

    def maxima(s, b):
        return [(s, "max", b, q) for q in range(QUADS)] + [(s, "mt", b)]

    def weights(s, b):
        out = []
        for u in range(8):
            out.append((s, "exp", b, u))
            if u == 6:
                out.append((s, "uev", b, 0))
            if u >= 2:
                out.append((s, "pv", b, u - 2))
        return out + [(s, "pv", b, 6), (s, "pv", b, 7), (s, "uev", b, 1), (s, "ut", b, 0), (s, "ut", b, 1)]

    down = [("M", "down", t, g) for t in range(TILES) for g in range(2)]
    route = [("M", k) for k in ("ln", "in", "logits", "route1", "e2", "route2")]
    up = [("M", "up", c) for c in range(NF // 2)]
    before_b = [("B", k) for k in ("ln", "in", "qkv", "pack")]
    return (
        merge(route + up, maxima("A", 0) + maxima("A", 1), before_b)
        + merge(weights("A", 0) + weights("A", 1), maxima("B", 0) + merge(weights("B", 0), maxima("B", 1)), down[:5])
        + merge([("A", "ot"), ("A", "proj"), ("A", "ln"), ("A0", "in"), ("A0", "qkv"), ("A0", "pack")],
                weights("B", 1), down[5:] + [("M", "out")])
        + [("B", "ot"), ("B", "proj")]
    )


SECTIONS = [
    (0, 1, {"A0": 0}),
    (1, 2, {"A0": 0, "A": -1}),
    (2, 3, {"A0": 0, "A": -1, "B": -2}),
    (3, PAIRS, {"A0": 0, "A": -1, "B": -2, "M": -3}),
    (PAIRS, PAIRS + 1, {"A": -1, "B": -2, "M": -3}),
    (PAIRS + 1, PAIRS + 2, {"B": -2, "M": -3}),
    (PAIRS + 2, PAIRS + 3, {"M": -3}),
]


def d_units(s, step, *args):
    if step == "max":
        return 4 if s == "A" else 3
    if step == "qkv":
        return 5 if s == "A0" else 3
    return int(step in ("in", "mt", "ut", "ot", "proj", "logits", "down"))


def a_units(s, step, *args):
    return int(step in ("exp", "up"))


def sections():
    out = []
    for lo, hi, offs in SECTIONS:
        steps = [x for x in turn_steps() if x[0] in offs]
        d_at, a_at, nd, na = {}, {}, 0, 0
        for x in steps:
            d_at[x], a_at[x] = nd, na
            nd, na = nd + d_units(*x), na + a_units(*x)
        assert nd % 2 == 0 and na % 2 == 0
        out.append((lo, hi, offs, steps, d_at, a_at, nd, na))
    return out


PACKS = 16 * (3 + 3 * J)


def program(nc, x, w_a, b_cols, bv_row, proj_a, pb_row, ln1, w_b, proj_b, ln2, router, w1, w2,
            ident, rope, mask, ones_rows, out):
    f32, f16 = mybir.dt.float32, mybir.dt.float16
    ALU, ACT, AX = mybir.AluOpType, mybir.ActivationFunctionType, mybir.AxisListType

    x_v = x.rearrange("(n t p) c -> n p t c", t=TILES, p=P)
    out_v = out.rearrange("(n t p) c -> n p t c", t=TILES, p=P)

    ctx = ExitStack()
    with ctx:
        def sb(name, shape, dt=f32):
            return ctx.enter_context(nc.sbuf_tensor(name, shape, dt))

        def sem(name):
            return ctx.enter_context(nc.semaphore(name))

        hid = sb("hid", [P, NF, PAIR])
        wa_f = hid[:, 0:2, :].rearrange("p a n -> p (a n)")[:, 0:5 * C].rearrange("p (g c) -> p g c", g=5)
        wb_f = hid[:, 2, 0:3 * C].rearrange("p (g c) -> p g c", g=3)
        rt_f = hid[:, 3, 0:E]
        w1_f = hid[:, 4:4 + E * F // PAIR, :].rearrange("p a n -> p (a n)")
        wa = sb("wa", [P, 2, 5, C], f16)
        wb = sb("wb", [P, 2, 3, C], f16)
        w1s = sb("w1s", [P, 2, E * F], f16)
        w2s = sb("w2s", [P, NF, C])
        rts = sb("rts", [P, 2, E], f16)
        projs = {"A": sb("proj_as", [P, C]), "B": sb("proj_bs", [P, C])}
        bcol = sb("bcol", [P, 4])
        bv = sb("bv", [P, C])
        pb = sb("pb", [P, C])
        lnw = {"B": sb("ln1s", [P, 1]), "M": sb("ln2s", [P, 1])}
        idf = sb("idf", [P, P])
        big = sb("big", [P, P], f16)
        ropes = sb("ropes", [P, 2, T])
        masks = sb("masks", [P, P], f16)
        epsc = sb("epsc", [P, TILES])
        halfc = sb("halfc", [P, TILES])
        order = sb("order", [P, TILES, E])

        L = {}
        for s in "AB":
            L[s] = dict(
                xs=sb(f"xs{s}", [P, 2, PAIR], f16),
                qs=sb(f"qs{s}", [P, 2, 2, PAIR], f16),
                qp=sb(f"qp{s}", [P, QUADS, PAIR], f16),
                kz=sb(f"kz{s}", [P, QUADS, J, PAIR], f16),
                v=sb(f"v{s}", [P, TILES, H, 32]),
                mx=sb(f"mx{s}", [P, 2, 2, H]),
                mt=sb(f"mt{s}", [H, 2, T], f16),
                pt=sb(f"pt{s}", [P, 4, J, T]),
                u=sb(f"u{s}", [P, QUADS, T]),
                rec=sb(f"rec{s}", [P, 2, H]),
                o=sb(f"o{s}", [P, TILES, C]),
                scratch=nc.dram_tensor(f"scratch{s}", [2, 2, P, PAIR], f16, kind="Internal").ap(),
            )
            L[s]["ot"] = L[s]["o"][:, :, :].rearrange("p t c -> p (t c)")
        xin = sb("xin", [P, TILES, C])
        xpb = sb("xpb", [P, TILES, C])
        rot = sb("rot", [P, 4, PAIR])
        ya = xpb
        x1r = sb("x1r", [P, TILES, C])
        x1 = sb("x1", [P, TILES, C])
        zb = sb("zb", [P, TILES, C])
        x2 = sb("x2", [P, TILES, C])
        x12 = sb("x12", [P, TILES, C])
        zm = sb("zm", [P, TILES, C])
        xsm = sb("xsm", [P, 2, PAIR], f16)
        tmp = sb("tmp", [P, 2, 4, C])
        part = sb("part", [P, 2, C])
        half = sb("half", [P, C])
        acc = sb("acc", [P, TILES, C])
        yout = zm
        stats = {k: sb(f"stats{k}", [P, TILES, 6]) for k in ("a", "b", "m", "o")}
        mv = {k: sb(f"mv{k}", [P, TILES, 2]) for k in ("a", "b", "m", "o")}
        ve = {k: sb(f"ve{k}", [P, TILES]) for k in ("a", "b", "m", "o")}
        rstd = {k: sb(f"rstd{k}", [P, TILES]) for k in ("a", "b", "m", "o")}
        lg = sb("lg", [P, TILES, E])
        best = sb("best", [P, 2, TILES])
        eq = sb("eq", [P, TILES, E])
        turn_ = sb("turn_", [P, TILES])
        sel = sb("sel", [P, 2, TILES, E])
        rest = sb("rest", [P, TILES, E])
        diff = sb("diff", [P, TILES])
        ed = sb("ed", [P, TILES])
        den = sb("den", [P, TILES])
        wts = sb("wts", [P, 2, TILES])
        gsel = sb("gsel", [P, 2, TILES, E])
        gate = sb("gate", [P, TILES, E])

        d_ps = [ctx.enter_context(nc.psum_tensor(f"d_ps{i}", [P, 512], f32)) for i in range(2)]
        a_ps = [ctx.enter_context(nc.psum_tensor(f"a_ps{i}", [P, 1024], f32)) for i in range(2)]
        u_ps = {s: ctx.enter_context(nc.psum_tensor(f"u_ps{s}", [P, 2, T], f32)) for s in "AB"}

        loaded = sem("loaded")
        rows_set = sem("rows_set")
        wait_carried = sem("wait_carried")
        consts = sem("consts")
        zeroed = sem("zeroed")
        split_w = sem("split_w")
        d_full, d_free = sem("d_full"), sem("d_free")
        a_full, a_free = sem("a_full"), sem("a_free")
        counted = []

        def csem(name, start=1):
            counted.append((sem(name), start))
            return counted[-1][0]

        x_loaded = csem("x_loaded")
        xpb_done = csem("xpb_done")
        split_done = csem("split_done")
        out_stored = csem("out_stored")
        out_done = csem("out_done")
        x1_done = csem("x1_done")
        S = {}
        for s in "AB":
            S[s] = {k: csem(f"{k}_{s}", 4 if k == "pv_done" else 1) for k in (
                "stored",
                "packed",
                "pv_done",
                "u_done",
            )}
            S[s]["mrows"] = [csem(f"mrows{b}_{s}") for b in range(2)]
        x12_done = csem("x12_done")
        masked = csem("masked")
        z_done = {s: csem(f"z_done{s}") for s in "BM"}
        stats_done = {k: csem(f"stats_done_{k}") for k in ("a", "b", "m", "o")}
        rstd_done = {k: csem(f"rstd_done_{k}") for k in ("a", "b", "m", "o")}
        diff_done, ed_done, gate_done = csem("diff_done"), csem("ed_done"), csem("gate_done")
        summed = csem("summed", 2)
        dve_link = {s: sem(f"dve_link_{s}") for s in ("A0", "A", "B", "M")}
        pool_link = {s: sem(f"pool_link_{s}") for s in ("A0", "A", "B", "M")}
        DVE_LINKS = {"A0": 1, "A": 5, "B": 9, "M": 18}
        POOL_LINKS = {"A0": 4, "A": 1, "B": 1, "M": 18}

        N_LOADS = 15
        plan = sections()

        class Now:

            def __init__(self, i, section, base, links):
                lo, _, offs, _, self.d_at, self.a_at, nd, na = section
                self.turn = {s: Turn(i, o) for s, o in offs.items()}
                self.d = Ring(2, (i - lo) * nd + base[0] if isinstance(i, int) else i * nd + (base[0] - lo * nd))
                self.a = Ring(2, (i - lo) * na + base[1] if isinstance(i, int) else i * na + (base[1] - lo * na))
                self.per, self.k = links, {s: 0 for s in offs}

            def d_done(self, *step, unit=0):
                return self.d.freed(self.d_at[step] + unit)

            def a_done(self, *step):
                return self.a.freed(self.a_at[step])

            def d_before(self):
                return self.d.base + 2

            def a_before(self):
                return self.a.base + 2

            def link(self, s):
                self.k[s] += 1
                return self.turn[s].raw(self.per[s], self.k[s])

            def end(self):
                for s, k in self.k.items():
                    assert self.per is None or k == self.per[s], (s, k, self.per[s])

        def walk(eng, do, links=None):
            base = [0, 0]
            for section in plan:
                lo, hi, _, steps, _, _, nd, na = section

                def turn(i):
                    now = Now(i, section, tuple(base), links)
                    for step in steps:
                        do(now, *step)
                    now.end()
                if hi - lo == 1:
                    turn(lo)
                else:
                    with eng.Fori(lo, hi) as i:
                        turn(i)
                base[0] += (hi - lo) * nd
                base[1] += (hi - lo) * na

        block = ctx.enter_context(nc.Block())

        @block.sync
        def _(sp):
            for dst, src in ((wa_f, w_a), (bcol[:, :], b_cols), (wb_f, w_b),
                             (idf[:, :], ident), (ropes[:, :, :], rope), (bv[:, :], bv_row.partition_broadcast(P)),
                             (pb[:, :], pb_row.partition_broadcast(P)), (projs["A"][:, :], proj_a),
                             (masks[:, :], mask), (lnw["B"][:, :], ln1), (projs["B"][:, :], proj_b),
                             (lnw["M"][:, :], ln2), (rt_f, router), (w1_f, w1),
                             (w2s[:, :, :], w2)):
                sp.dma_start(dst, src).then_inc(loaded, 16)
            sp.wait_ge(zeroed, 2)
            for s in "AB":
                sp.dma_start(L[s]["kz"][DATA:ROWS, :, :, :], ones_rows).then_inc(rows_set, 16)

            def do(now, stage, step, *args):
                t = now.turn[stage]
                s = "A" if stage == "A0" else stage
                if stage == "A0" and step == "in":
                    sp.wait_ge(d_free, now.d_before())
                    sp.sem_inc(wait_carried, 1)
                    sp.wait_ge(xpb_done, t(1, 0))
                    sp.sem_inc(wait_carried, 1)
                    sp.dma_start(xin[:, :, :], x_v[t.index(), :, :, :]).then_inc(x_loaded, 16)
                if step == "pack":
                    B, Z = L[s], S[s]
                    sp.wait_ge(Z["packed"], t(PACKS, 0))
                    sp.sem_inc(wait_carried, 1)
                    for w in range(2):
                        if s == "A":
                            sp.wait_ge(split_done, t(2, w + 1))
                        else:
                            sp.wait_ge(d_free, now.d_done("B", "qkv", unit=w))
                        sp.dma_start(B["scratch"][w].rearrange("h p n -> p h n"), B["qs"][:, w, :, :]).then_inc(Z["stored"], 16)
                    sp.wait_ge(Z["pv_done"], t(16, 3))
                    sp.sem_inc(wait_carried, 1)
                    sp.wait_ge(Z["stored"], t(32, 32))
                    q_src, k_src = B["scratch"][0], B["scratch"][1]
                    for c, h in ((0, 0), (1, 0), (2, 1)):
                        sp.dma_start(B["qp"][32 * c:32 * c + 32, :, :],
                                     q_src[h].rearrange("(q r) n -> r q n", q=QUADS)).then_inc(Z["packed"], 16)
                    for c, h in ((0, 0), (1, 1), (2, 0)):
                        for j in range(J):
                            r = 32 * c + HD * j
                            sp.dma_start(B["kz"][r:r + HD, :, j, :],
                                         k_src[h].rearrange("(q j d) n -> j d q n", q=QUADS, j=J)[j]).then_inc(Z["packed"], 16)
                if step == "mt":
                    b, = args
                    sp.wait_ge(d_free, now.d_done(s, "mt", b))
                    for q in range(QUADS):
                        sp.dma_start(L[s]["qp"][DATA:ROWS, q, b * T:(b + 1) * T], L[s]["mt"][:, b, :]).then_inc(S[s]["mrows"][b], 16)
                if step == "out":
                    sp.wait_ge(out_done, t(1, 1))
                    sp.sem_inc(wait_carried, 1)
                    sp.dma_start(out_v[t.index(), :, :, :], yout[:, :, :]).then_inc(out_stored, 16)

            for q, start in counted[0::4]:
                sp.sem_inc(q, start)
            walk(sp, do)
            sp.wait_ge(out_stored, 1 + 16 * PAIRS)

        @block.gpsimd
        def _(pool):
            for q, start in counted[1::4]:
                pool.sem_inc(q, start)
            pool.memset(epsc[:, :], EPS).then_inc(consts, 1)
            pool.memset(halfc[:, :], -0.5).then_inc(consts, 1)
            for e in range(E):
                pool.memset(order[:, :, e:e + 1], float(E - e))
            pool.memset(L["A"]["v"][:, :, :, :], 0.0).then_inc(consts, 1)
            pool.memset(L["B"]["v"][:, :, :, :], 0.0).then_inc(consts, 1)
            pool.wait_ge(consts, 4)
            for s in "AB":
                pool.memset(L[s]["v"][:, :, :, HD:HD + 1], 1.0).then_inc(consts, 1)
            pool.wait_ge(loaded, 16 * N_LOADS)
            pool.tensor_scalar(big[:, :], idf[:, :], DIAG, 0.0, ALU.mult, ALU.add).then_inc(consts, 1)

            def do(now, stage, step, *args):
                t = now.turn[stage]
                s = "A" if stage == "A0" else stage

                def rsqrt(k, per_pair_credit=True):
                    pool.wait_ge(stats_done[k], t(1, 1))
                    pool.tensor_tensor(ve[k][:, :], mv[k][:, :, 1], epsc[:, :], ALU.add).then_inc(pool_link[stage], 1)
                    pool.wait_ge(pool_link[stage], now.link(stage))
                    pool.tensor_tensor(rstd[k][:, :], ve[k][:, :], halfc[:, :], ALU.pow).then_inc(rstd_done[k], 1)

                if stage == "A0" and step == "in":
                    pool.wait_ge(x_loaded, t(16, 16))
                    pool.wait_ge(x1_done, t(1, 0))
                    pool.tensor_tensor(xpb[:, :, :], xin[:, :, :], pb[:, :].unsqueeze(1).to_broadcast([P, TILES, C]), ALU.add).then_inc(xpb_done, 1)
                if stage == "A0" and step == "qkv":
                    for w in range(2):
                        pool.wait_ge(d_free, now.d_done("A0", "qkv", unit=2 * w + 1))
                        pool.wait_ge(S["A"]["stored"], t(32, 0))
                        pool.tensor_tensor(L["A"]["qs"][:, w, 0, :], rot[:, 2 * w, :], rot[:, 2 * w + 1, :], ALU.add).then_inc(pool_link["A0"], 1)
                        pool.wait_ge(pool_link["A0"], now.link("A0"))
                        pool.tensor_tensor(rot[:, 2 * w, :], rot[:, 2 * w, :], rot[:, 2 * w + 1, :], ALU.add).then_inc(pool_link["A0"], 1)
                        pool.wait_ge(pool_link["A0"], now.link("A0"))
                        pool.tensor_tensor(L["A"]["qs"][:, w, 1, :], rot[:, 2 * w, :], L["A"]["qs"][:, w, 0, :], ALU.subtract).then_inc(split_done, 1)
                if (s, step) == ("A", "ln"):
                    rsqrt("a")
                if (s, step) == ("B", "ln"):
                    rsqrt("b")
                if (s, step) == ("M", "ln"):
                    rsqrt("m")
                if (s, step) == ("M", "out"):
                    rsqrt("o")
                if (s, step) == ("B", "proj"):
                    pool.wait_ge(d_free, now.d_done("B", "proj"))
                    pool.tensor_tensor(x12[:, :, :], x2[:, :, :], x1r[:, :, :], ALU.add).then_inc(x12_done, 1)
                if (s, step) == ("B", "exp"):
                    b, u = args
                    kt = u % 2
                    pool.wait_ge(a_free, now.a_done("B", "exp", b, u))
                    pool.sem_inc(wait_carried, 1)
                    v = L["B"]["pt"][:, u % 4, :, kt * P:(kt + 1) * P]
                    pool.affine_select(out=v, in_=v, pattern=[[0, J], [1, P]], compare_op=ALU.is_ge, fill=0.0,
                                       base=0, channel_multiplier=-1).then_inc(masked, 1)
                if (s, step) == ("M", "down"):
                    tile, g = args
                    n = 2 * tile + g
                    pool.wait_ge(d_free, now.d_done("M", "down", tile, g))
                    if n == 0:
                        pool.wait_ge(out_done, t(1, 0))
                        pool.wait_ge(x12_done, t(1, 1))
                    tm = tmp[:, n % 2]
                    pool.tensor_tensor(part[:, :, :], tm[:, 0:2, :], tm[:, 2:4, :], ALU.add).then_inc(pool_link["M"], 1)
                    pool.wait_ge(pool_link["M"], now.link("M"))
                    pool.tensor_tensor(half[:, :], part[:, 0, :], part[:, 1, :], ALU.add).then_inc(pool_link["M"], 1)
                    pool.wait_ge(pool_link["M"], now.link("M"))
                    pool.tensor_tensor(acc[:, tile, :], half[:, :], x12[:, tile, :] if g == 0 else acc[:, tile, :], ALU.add).then_inc(summed, 1)
                    pool.wait_ge(summed, t(8, n + 2))

            walk(pool, do, POOL_LINKS)

        @block.scalar
        def _(act):
            for q, start in counted[2::4]:
                act.sem_inc(q, start)
            act.sem_inc(a_free, 2)

            def do(now, stage, step, *args):
                t = now.turn[stage]
                s = "A" if stage == "A0" else stage
                if step == "exp":
                    b, u = args
                    B, Z = L[s], S[s]
                    slot, count = now.a.next()
                    n = 8 * b + u
                    act.wait_ge(a_full, count)
                    act.wait_ge(Z["pv_done"], t(16, n))
                    if s == "B" and u % 2:
                        dst, src = B["pt"][:, u % 4, :, P:T], a_ps[slot][:, 0:J * P].rearrange("p (j n) -> p j n", j=J)
                    else:
                        dst, src = B["pt"][:, u % 4, :, :], a_ps[slot][:, :].rearrange("p (j n) -> p j n", j=J)
                    act.activation(dst, src, ACT.Exp, scale=SCALE).then_inc(a_free, 1)
                if step == "uev":
                    b, half_ = args
                    B, Z = L[s], S[s]
                    act.wait_ge(Z["pv_done"], t(16, 8 * b + 4 * half_ + 4 + 3))
                    act.wait_ge(d_free, now.d_done(s, "ut", 0, 1) if b else now.d_before())
                    act.activation(B["u"][:, 2 * half_:2 * half_ + 2, :], u_ps[s][:, :, :], ACT.Copy).then_inc(Z["u_done"], 1)
                if step == "e2":
                    act.wait_ge(diff_done, t(1, 1))
                    act.wait_ge(gate_done, t(1, 0))
                    act.activation(ed[:, :], diff[:, :], ACT.Exp).then_inc(ed_done, 1)
                if step == "up":
                    c, = args
                    slot, count = now.a.next()
                    act.wait_ge(a_full, count)
                    if c == 0:
                        act.wait_ge(d_free, now.d_before())
                    act.activation(hid[:, 2 * c:2 * c + 2, :], a_ps[slot][:, :].rearrange("p (c n) -> p c n", c=2), ACT.Gelu).then_inc(a_free, 1)

            walk(act, do)

        @block.tensor
        def _(pe):
            for q, start in counted[3::4]:
                pe.sem_inc(q, start)
            pe.wait_ge(loaded, 16 * N_LOADS)
            pe.wait_ge(rows_set, 32)
            pe.wait_ge(consts, 7)
            pe.wait_ge(split_w, 8)

            def three(dst, wide, moving):
                for n, (a, b) in enumerate(((0, 0), (1, 0), (0, 1))):
                    last = pe.matmul(dst, wide(a), moving(b), start=n == 0, stop=n == 2)
                return last

            def turned(now, src):
                slot, count = now.d.next()
                pe.wait_ge(d_free, count)
                for i in range(TILES):
                    last = pe.transpose(d_ps[slot][:, i * P:(i + 1) * P], src[:, i, :], idf[:, :])
                last.then_inc(d_full, 1)

            def do(now, stage, step, *args):
                t = now.turn[stage]
                s = "A" if stage == "A0" else stage
                if step == "in":
                    if s == "A":
                        pe.wait_ge(x_loaded, t(16, 16))
                        turned(now, xin)
                    else:
                        pe.wait_ge(z_done[s], t(1, 1))
                        turned(now, zb if s == "B" else zm)
                if step == "qkv":
                    xs, w = L[s]["xs"], wa if s == "A" else wb
                    pe.wait_ge(d_free, now.d_done(stage, "in"))
                    n_t = 4 if s == "A" else 2
                    for g in range(n_t):
                        slot, count = now.d.next()
                        pe.wait_ge(d_free, count)
                        three(d_ps[slot][:, :], lambda a: w[:, a, g, :], lambda b: xs[:, b, :]).then_inc(d_full, 1)
                    slot, count = now.d.next()
                    pe.wait_ge(d_free, count)
                    for i in range(TILES):
                        last = three(d_ps[slot][:, i * P:(i + 1) * P], lambda a: xs[:, a, i * P:(i + 1) * P],
                                     lambda b: w[:, b, n_t, :])
                    last.then_inc(d_full, 1)
                if step == "max":
                    b, q = args
                    B = L[s]
                    if b == 0 and q == 0:
                        pe.wait_ge(S[s]["packed"], t(PACKS, PACKS))
                    for qt in range(2):
                        at = b * T + qt * P
                        wide = B["qp"][0:DATA, q, at:at + P]
                        if s == "B" and qt == 0:
                            slot, count = now.d.next()
                            pe.wait_ge(d_free, count)
                            pe.matmul(d_ps[slot][:, :], wide, B["kz"][0:DATA, q, :, b * T:b * T + P], start=True, stop=False)
                            pe.matmul(d_ps[slot][:, :], big[:, :], masks[:, :].unsqueeze(1).to_broadcast([P, J, P]),
                                      start=False, stop=True).then_inc(d_full, 1)
                            continue
                        for h in range(2):
                            slot, count = now.d.next()
                            pe.wait_ge(d_free, count)
                            last = pe.matmul(d_ps[slot][:, :], wide, B["kz"][0:DATA, q, 2 * h:2 * h + 2, b * T:(b + 1) * T],
                                             start=True, stop=s == "A")
                            if s == "B":
                                last = pe.matmul(d_ps[slot][:, :].rearrange("p (j n) -> p j n", j=2)[:, :, P:T], big[:, :],
                                                 masks[:, :].unsqueeze(1).to_broadcast([P, 2, P]), start=False, stop=True)
                            last.then_inc(d_full, 1)
                if step == "mt":
                    b, = args
                    pe.wait_ge(d_free, now.d_done(s, "max", b, QUADS - 1, unit=3 if s == "A" else 2))
                    slot, count = now.d.next()
                    pe.wait_ge(d_free, count)
                    for qt in range(2):
                        last = pe.transpose(d_ps[slot][0:H, qt * P:(qt + 1) * P], L[s]["mx"][:, b, qt, :], idf[:, :])
                    last.then_inc(d_full, 1)
                if step == "exp":
                    b, u = args
                    B = L[s]
                    q, kt = u // 2, u % 2
                    if u == 0:
                        pe.wait_ge(S[s]["mrows"][b], t(64, 64))
                    slot, count = now.a.next()
                    pe.wait_ge(a_free, count)
                    first = P if s == "B" and kt else 0
                    n = T - first
                    for j in range(J):
                        last = pe.matmul(a_ps[slot][:, j * n:(j + 1) * n], B["kz"][0:ROWS, q, j, b * T + kt * P:b * T + (kt + 1) * P],
                                         B["qp"][0:ROWS, q, b * T + first:(b + 1) * T], start=True, stop=True)
                    last.then_inc(a_full, 1)
                if step == "pv":
                    b, u = args
                    B, Z = L[s], S[s]
                    q, kt = u // 2, u % 2
                    if b == 0 and u == 0:
                        pe.wait_ge(d_free, now.d_before() if s == "A" else now.d_done("B", "qkv", unit=2))
                    if s == "A":
                        pe.wait_ge(a_free, now.a_done("A", "exp", b, u))
                    else:
                        pe.wait_ge(masked, t(16, 8 * b + u + 1))
                    if u % 4 == 0:
                        pe.wait_ge(Z["u_done"], t(4, 2 * b + u // 4))
                    first = P if s == "B" and kt else 0
                    for j in range(J):
                        last = pe.matmul(u_ps[s][32 * j:32 * j + 32, q % 2, first:T], B["v"][:, 2 * b + kt, J * q + j, :],
                                         B["pt"][:, u % 4, j, first:T], start=kt == 0, stop=kt == 1)
                    last.then_inc(Z["pv_done"], 1)
                if step == "ut":
                    b, qt = args
                    pe.wait_ge(S[s]["u_done"], t(4, 2 * b + 2))
                    slot, count = now.d.next()
                    pe.wait_ge(d_free, count)
                    for q in range(QUADS):
                        last = pe.transpose(d_ps[slot][:, q * P:(q + 1) * P], L[s]["u"][:, q, qt * P:(qt + 1) * P], idf[:, :])
                    last.then_inc(d_full, 1)
                if step == "ot":
                    pe.wait_ge(d_free, now.d_done(s, "ut", 1, 1))
                    turned(now, L[s]["o"])
                if step == "proj":
                    pe.wait_ge(d_free, now.d_done(s, "ot"))
                    slot, count = now.d.next()
                    pe.wait_ge(d_free, count)
                    for i in range(TILES):
                        last = pe.matmul(d_ps[slot][:, i * P:(i + 1) * P], L[s]["ot"][:, i * P:(i + 1) * P], projs[s][:, :],
                                         start=True, stop=True)
                    last.then_inc(d_full, 1)
                if step == "logits":
                    pe.wait_ge(d_free, now.d_done("M", "in"))
                    slot, count = now.d.next()
                    pe.wait_ge(d_free, count)
                    for i in range(TILES):
                        last = three(d_ps[slot][:, i * E:(i + 1) * E], lambda a: xsm[:, a, i * P:(i + 1) * P], lambda b: rts[:, b, :])
                    last.then_inc(d_full, 1)
                if step == "up":
                    c, = args
                    slot, count = now.a.next()
                    pe.wait_ge(a_free, count)
                    for k in range(2):
                        f = 2 * c + k
                        last = three(a_ps[slot][:, k * PAIR:(k + 1) * PAIR], lambda a: w1s[:, a, f * P:(f + 1) * P], lambda b: xsm[:, b, :])
                    last.then_inc(a_full, 1)
                if step == "down":
                    tile, g = args
                    if g == 0:
                        pe.wait_ge(a_free, now.a_done("M", "up", NF // 2 - 1))
                    slot, count = now.d.next()
                    pe.wait_ge(d_free, count)
                    for e in range(4):
                        for k in range(2):
                            f = 2 * (4 * g + e) + k
                            last = pe.matmul(d_ps[slot][:, e * C:(e + 1) * C], hid[:, f, tile * P:(tile + 1) * P], w2s[:, f, :],
                                             start=k == 0, stop=k == 1)
                    last.then_inc(d_full, 1)

            walk(pe, do)

        @block.vector
        def _(dve):
            dve.sem_inc(d_free, 2)
            for s in "AB":
                dve.memset(L[s]["kz"][:, :, :, :], 0.0).then_inc(zeroed, 1)
            dve.wait_ge(loaded, 16 * N_LOADS)
            k = 0
            for f, hl in ((wa_f, lambda h: wa[:, h, :, :]), (wb_f, lambda h: wb[:, h, :, :]),
                          (w1_f, lambda h: w1s[:, h, :]), (rt_f, lambda h: rts[:, h, :])):
                dve.tensor_copy(hl(0), f).then_inc(split_w, 1)
                k += 1
                dve.wait_ge(split_w, k)
                dve.tensor_tensor(hl(1), f, hl(0), ALU.subtract).then_inc(split_w, 1)
                k += 1
            dve.wait_ge(consts, 7)

            def ring(now):
                slot, count = now.d.next()
                dve.wait_ge(d_full, count)
                return d_ps[slot]

            def do(now, stage, step, *args):
                t = now.turn[stage]
                s = "A" if stage == "A0" else stage
                link = dve_link[stage]

                def stats_of(k, src):
                    for i in range(TILES):
                        last = dve.bn_stats(stats[k][:, i, :], src[:, i, :])
                    last.then_inc(link, 1)
                    dve.wait_ge(link, now.link(stage))
                    dve.sem_inc(wait_carried, 1)
                    for i in range(TILES):
                        last = dve.bn_aggr(mv[k][:, i, :], stats[k][:, i, :])
                    last.then_inc(stats_done[k], 1)

                def normalised(k, dst, src, done):
                    dve.wait_ge(rstd_done[k], t(1, 1))
                    for i in range(TILES):
                        last = dve.tensor_scalar(dst[:, i, :], src[:, i, :], mv[k][:, i, 0:1], rstd[k][:, i:i + 1], ALU.subtract, ALU.mult)
                    last.then_inc(done, 1)

                if step == "in":
                    xs = xsm if s == "M" else L[s]["xs"]
                    if s == "M":
                        dve.wait_ge(a_free, now.a_before())
                    ps = ring(now)
                    if s == "A":
                        dve.tensor_copy(xs[:, 0, :], ps[:, :]).then_inc(link, 1)
                        dve.wait_ge(link, now.link(stage))
                        dve.tensor_tensor(xs[:, 1, :], ps[:, :], xs[:, 0, :], ALU.subtract).then_inc(d_free, 1)
                    else:
                        dve.tensor_scalar(xs[:, 0, :], ps[:, :], lnw[s][:, 0:1], None, ALU.mult).then_inc(link, 1)
                        dve.wait_ge(link, now.link(stage))
                        dve.scalar_tensor_tensor(xs[:, 1, :], ps[:, :], lnw[s][:, 0:1], xs[:, 0, :], ALU.mult, ALU.subtract).then_inc(d_free, 1)
                if stage == "A0" and step == "qkv":
                    dve.wait_ge(split_done, t(2, 0))
                    for g in range(4):
                        ps = ring(now)
                        dve.scalar_tensor_tensor(rot[:, g, :].rearrange("p (b n) -> p b n", b=2), ps[:, :].rearrange("p (b n) -> p b n", b=2),
                                                 bcol[:, g:g + 1], ropes[:, g % 2, :].unsqueeze(1).to_broadcast([P, 2, T]),
                                                 ALU.add, ALU.mult).then_inc(d_free, 1)
                if (s, step) == ("B", "qkv"):
                    dve.wait_ge(S["B"]["stored"], t(32, 0))
                    for g in range(2):
                        ps = ring(now)
                        qs = L["B"]["qs"]
                        dve.tensor_copy(qs[:, g, 0, :], ps[:, :]).then_inc(link, 1)
                        dve.wait_ge(link, now.link(stage))
                        dve.tensor_tensor(qs[:, g, 1, :], ps[:, :], qs[:, g, 0, :], ALU.subtract).then_inc(d_free, 1)
                if step == "qkv":
                    dve.wait_ge(S[s]["pv_done"], t(16, 3))
                    ps = ring(now)
                    v = L[s]["v"]
                    for i in range(TILES):
                        src = ps[:, i * P:(i + 1) * P].rearrange("p (h d) -> p h d", d=HD)
                        if s == "A":
                            last = dve.tensor_tensor(v[:, i, :, 0:HD], src, bv[:, :].rearrange("p (h d) -> p h d", d=HD), ALU.add)
                        else:
                            last = dve.tensor_copy(v[:, i, :, 0:HD], src)
                    last.then_inc(d_free, 1)
                if step == "max":
                    b, q = args
                    mx = L[s]["mx"]
                    for qt in range(2):
                        if s == "B" and qt == 0:
                            ps = ring(now)
                            dve.tensor_reduce(mx[:, b, 0, J * q:J * q + J], ps[:, :].rearrange("p (j n) -> p j n", j=J), AX.X, ALU.max).then_inc(d_free, 1)
                            continue
                        for h in range(2):
                            ps = ring(now)
                            at = J * q + 2 * h
                            dve.tensor_reduce(mx[:, b, qt, at:at + 2], ps[:, :].rearrange("p (j n) -> p j n", j=2), AX.X, ALU.max).then_inc(d_free, 1)
                if step == "mt":
                    b, = args
                    for bb in range(2):
                        dve.wait_ge(S[s]["mrows"][bb], t(64, 0))
                    ps = ring(now)
                    dve.tensor_scalar(L[s]["mt"][:, b, :], ps[0:H, 0:T], -1.0 / MSCALE, None, ALU.mult).then_inc(d_free, 1)
                if step == "ut":
                    b, qt = args
                    B = L[s]
                    ps = ring(now)
                    v = ps[:, :].rearrange("p (h r) -> p h r", r=32)
                    dve.reciprocal(B["rec"][:, qt, :], v[:, :, HD]).then_inc(link, 1)
                    dve.wait_ge(link, now.link(stage))
                    dve.tensor_tensor(B["o"][:, 2 * b + qt, :].rearrange("p (h d) -> p h d", d=HD), v[:, :, 0:HD],
                                      B["rec"][:, qt, :].unsqueeze(2).to_broadcast([P, H, HD]), ALU.mult).then_inc(d_free, 1)
                if step == "ot":
                    ps = ring(now)
                    dve.tensor_copy(L[s]["ot"], ps[:, :]).then_inc(d_free, 1)
                if step == "proj":
                    if s == "A":
                        dve.wait_ge(xpb_done, t(1, 1))
                        dst, res = ya, xpb
                    else:
                        dve.wait_ge(x12_done, t(1, 0))
                        dst, res = x2, x1r
                    ps = ring(now)
                    dve.tensor_tensor(dst[:, :, :], ps[:, :].rearrange("p (t c) -> p t c", t=TILES), res[:, :, :], ALU.add).then_inc(d_free, 1)
                if (s, step) == ("A", "ln"):
                    dve.wait_ge(d_free, now.d_done("A", "proj"))
                    stats_of("a", ya)
                    normalised("a", x1, ya, x1_done)
                if (s, step) == ("B", "ln"):
                    dve.wait_ge(x1_done, t(1, 1))
                    stats_of("b", x1)
                    dve.wait_ge(x12_done, t(1, 0))
                    dve.tensor_copy(x1r[:, :, :], x1[:, :, :]).then_inc(link, 1)
                    dve.wait_ge(link, now.link(stage))
                    normalised("b", zb, x1, z_done["B"])
                if (s, step) == ("M", "ln"):
                    dve.wait_ge(d_free, now.d_before())
                    stats_of("m", x2)
                    dve.wait_ge(out_stored, t(16, 0))
                    normalised("m", zm, x2, z_done["M"])
                if step == "logits":
                    ps = ring(now)
                    dve.tensor_copy(lg[:, :, :], ps[:, 0:TILES * E].rearrange("p (t e) -> p t e", e=E)).then_inc(d_free, 1)

                def wide(ap):
                    return ap.unsqueeze(2).to_broadcast([P, TILES, E])

                def choose(n, src):
                    dve.tensor_reduce(best[:, n, :], src, AX.X, ALU.max).then_inc(link, 1)
                    dve.wait_ge(link, now.link(stage))
                    dve.tensor_tensor(eq[:, :, :], src, wide(best[:, n, :]), ALU.is_ge).then_inc(link, 1)
                    dve.wait_ge(link, now.link(stage))
                    dve.tensor_tensor(eq[:, :, :], eq[:, :, :], order[:, :, :], ALU.mult).then_inc(link, 1)
                    dve.wait_ge(link, now.link(stage))
                    dve.tensor_reduce(turn_[:, :], eq[:, :, :], AX.X, ALU.max).then_inc(link, 1)
                    dve.wait_ge(link, now.link(stage))
                    dve.tensor_tensor(sel[:, n, :, :], eq[:, :, :], wide(turn_[:, :]), ALU.is_equal).then_inc(link, 1)
                    dve.wait_ge(link, now.link(stage))

                if step == "route1":
                    dve.wait_ge(d_free, now.d_done("M", "logits"))
                    choose(0, lg[:, :, :])
                    dve.scalar_tensor_tensor(rest[:, :, :], sel[:, 0, :, :], -3.0e38, lg[:, :, :], ALU.mult, ALU.add).then_inc(link, 1)
                    dve.wait_ge(link, now.link(stage))
                    choose(1, rest[:, :, :])
                    dve.tensor_tensor(diff[:, :], best[:, 1, :], best[:, 0, :], ALU.subtract).then_inc(diff_done, 1)
                if step == "route2":
                    dve.wait_ge(ed_done, t(1, 1))
                    dve.tensor_scalar(den[:, :], ed[:, :], 1.0, None, ALU.add).then_inc(link, 1)
                    dve.wait_ge(link, now.link(stage))
                    dve.reciprocal(wts[:, 0, :], den[:, :]).then_inc(link, 1)
                    dve.wait_ge(link, now.link(stage))
                    dve.tensor_tensor(wts[:, 1, :], wts[:, 0, :], ed[:, :], ALU.mult).then_inc(link, 1)
                    dve.wait_ge(link, now.link(stage))
                    for n in range(2):
                        last = dve.tensor_tensor(gsel[:, n, :, :], sel[:, n, :, :], wide(wts[:, n, :]), ALU.mult)
                    last.then_inc(link, 1)
                    dve.wait_ge(link, now.link(stage))
                    dve.tensor_tensor(gate[:, :, :], gsel[:, 0, :, :], gsel[:, 1, :, :], ALU.add).then_inc(gate_done, 1)
                    dve.wait_ge(gate_done, t(1, 1))
                if step == "down":
                    tile, g = args
                    n = 2 * tile + g
                    dve.wait_ge(summed, t(8, n))
                    ps = ring(now)
                    dve.tensor_tensor(tmp[:, n % 2], ps[:, :].rearrange("p (e c) -> p e c", e=4),
                                      gate[:, tile, 4 * g:4 * g + 4].unsqueeze(2).to_broadcast([P, 4, C]), ALU.mult).then_inc(d_free, 1)
                if (s, step) == ("M", "out"):
                    dve.wait_ge(summed, t(8, 8 + 1))
                    stats_of("o", acc)
                    normalised("o", yout, acc, out_done)

            walk(dve, do, DVE_LINKS)


_INS = ["x", "w_a", "b_cols", "bv_row", "proj_a", "pb_row", "ln1", "w_b", "proj_b", "ln2", "router", "w1", "w2",
        "ident", "rope", "mask", "ones_rows"]


def constants():
    pos = np.arange(T, dtype=np.float32)
    inv = (1.0 / np.float32(10000.0) ** (np.arange(0, HD, 2, dtype=np.float32) / np.float32(HD))).astype(np.float32)
    freqs = pos[None, :] * inv[:, None]
    cos, sin = np.cos(freqs), np.sin(freqs)
    d = np.arange(P) % HD
    sign = np.where(d % 2 == 0, -1.0, 1.0)[:, None].astype(np.float32)
    rope = np.stack([cos[d // 2], sin[d // 2] * sign], axis=1).astype(np.float32)
    q, k = np.arange(P)[:, None], np.arange(P)[None, :]
    mask = np.where(k > q, -MASKED, 0.0).astype(np.float16)
    rows = np.zeros((H, QUADS, J, PAIR), np.float16)
    for h in range(H):
        rows[h, h // J, h % J, :] = MSCALE
    return {"ident": np.eye(P, dtype=np.float32), "rope": rope, "mask": mask, "ones_rows": rows}


def kernel(L0_attn_x, L0_attn_qkv_w, L0_attn_qkv_b, L0_attn_proj_w, L0_attn_proj_b, L0_ffn_ln1_w,
           L0_ffn_c_attn_w, L0_ffn_c_proj_w, L0_ffn_ln2_w, L0_ffn_router_w, L0_ffn_w1, L0_ffn_w2):
    import concourse.bacc as bacc
    from concourse.bass_utils import run_bass_kernel_spmd

    swapped = np.arange(C) ^ 1
    w = np.asarray(L0_attn_qkv_w).reshape(3, C, C)
    bias = np.asarray(L0_attn_qkv_b).reshape(3, C)
    arrays = {
        "x": np.asarray(L0_attn_x).reshape(SEQ * T, C),
        "w_a": np.stack([w[0].T, w[0][swapped].T, w[1].T, w[1][swapped].T, w[2].T], axis=1),
        "b_cols": np.stack([bias[0], bias[0][swapped], bias[1], bias[1][swapped]], axis=1),
        "bv_row": bias[2],
        "proj_a": np.asarray(L0_attn_proj_w).T,
        "pb_row": np.asarray(L0_attn_proj_b),
        "ln1": np.asarray(L0_ffn_ln1_w).reshape(C, 1),
        "w_b": np.asarray(L0_ffn_c_attn_w).reshape(C, 3, C),
        "proj_b": np.asarray(L0_ffn_c_proj_w),
        "ln2": np.asarray(L0_ffn_ln2_w).reshape(C, 1),
        "router": np.asarray(L0_ffn_router_w),
        "w1": np.asarray(L0_ffn_w1),
        "w2": np.asarray(L0_ffn_w2).reshape(NF, P, C).transpose(1, 0, 2),
        **constants(),
    }
    arrays = {k: np.ascontiguousarray(v) for k, v in arrays.items()}
    nc = bacc.Bacc("TRN2", target_bir_lowering=False, num_devices=1)
    args = [nc.dram_tensor(f"in_{k}", arrays[k].shape, mybir.dt.from_np(arrays[k].dtype), kind="ExternalInput").ap() for k in _INS]
    out = nc.dram_tensor("out_0", (SEQ * T, C), mybir.dt.float32, kind="ExternalOutput").ap()
    program(nc, *args, out)
    r = run_bass_kernel_spmd(nc, [{f"in_{k}": arrays[k] for k in _INS}], core_ids=[0])
    return r.results[0]["out_0"].reshape(SEQ, T, C)
```

```python
import numpy as np
import concourse.bass as bass
from concourse import mybir
from contextlib import ExitStack

C = 128
SEQ, T = 32, 256
H, HD = 16, 8
E, F = 8, 256
P = 128
QUADS, J = 4, 4
PAIR = 2 * T
PAIRS = SEQ * T // PAIR
TILES = PAIR // P
NF = E * F // P
DATA = 3 * 32
ROWS = DATA + H
MSCALE = 64.0
MASKED = 60000.0
DIAG = 1024.0
EPS = 1e-5
D_SLOTS, A_SLOTS = 4, 2
SCALE = HD ** -0.5


class Ring:

    def __init__(self, slots, first, base):
        self.slots, self.first, self.base, self.used = slots, first, base, 0

    def next(self):
        i = self.used
        self.used += 1
        return (self.first + i) % self.slots, self.base + (i + 1)

    def freed(self, i):
        return self.base + (i + 1 + self.slots)


class Turn:

    def __init__(self, i, off):
        self.i, self.off = i, off

    def __call__(self, per, k):
        return self.i * per + (self.off * per + k + 1)

    def raw(self, per, k):
        return self.i * per + (self.off * per + k)

    def index(self):
        return self.i + self.off if self.off else self.i


TURNS = {
    "fill": """
B ln | B z | A max 0 0 0 | A max 0 0 1 | B in | A max 0 1 0 | A max 0 1 1 | B qk | A max 0 2 0 | B stow
B v | A0 load | B pack 0 | A max 0 2 1 | A max 0 3 0 | A max 0 3 1 | A max 1 0 0 | A mt 0 | A max 1 0 1
A max 1 1 0 | A max 1 1 1 | A max 1 2 0 | A exp 0 0 | B pack 1 | A max 1 2 1 | A exp 0 1 | A max 1 3 0
A exp 0 2 | A max 1 3 1 | A exp 0 3 | A pv 0 0 | B pack 2 | B max 0 0 0 | B max 0 0 1 | A exp 0 4
B max 0 1 0 | B max 0 1 1 | A exp 0 5 | B max 0 2 0 | B max 0 2 1 | A mt 1 | B max 0 3 0 | A pv 0 1
A exp 0 6 | A exp 0 7 | B max 0 3 1 | B max 1 0 0 | A pv 0 2 | B mt 0 | A pv 0 3 | B max 1 0 1
B max 1 1 0 | A exp 1 0 | B exp 0 0 | B exp 0 1 | B max 1 1 1 | A0 in | B exp 0 2 | A exp 1 1
B max 1 2 0 | A ut 0 0 | B pv 0 0 | A exp 1 2 | B exp 0 3 | A0 qk | A exp 1 3 | B exp 0 4 | B max 1 2 1
B pv 0 1 | A ut 0 1 | B exp 0 5 | A pv 1 0 | B max 1 3 0 | B exp 0 6 | B exp 0 7 | B max 1 3 1 | A exp 1 4
B pv 0 2 | B mt 1 | A exp 1 5 | B pv 0 3 | A pv 1 1 | A0 split | A exp 1 6 | B exp 1 0 | A pv 1 2
A exp 1 7 | B ut 0 0 | B exp 1 1 | B ut 0 1 | A pv 1 3 | A0 stow | B exp 1 2 | B pv 1 0 | B exp 1 3
A ut 1 0 | B exp 1 4 | A ut 1 1 | A0 pack 0 | B exp 1 5 | A ot | B pv 1 1 | A proj | B exp 1 6 | B exp 1 7
A ln | B pv 1 2 | A0 v | A out | B pv 1 3 | A0 pack 1 | B ut 1 0 | B ut 1 1 | A0 pack 2 | B ot | A0 xpb
B proj | B x12
""",
    "full": """
M ln | B ln | A max 0 0 0 | B z | M z | A max 0 0 1 | B in | A max 0 1 0 | M in | B qk | M up 0
A max 0 1 1 | A max 0 2 0 | B v | B stow | A max 0 2 1 | M up 1 | A max 0 3 0 | B pack 0 | M logits
A max 0 3 1 | M up 2 | A max 1 0 0 | A mt 0 | A max 1 0 1 | M up 3 | M route1 | M up 4 | M up 5 | B pack 1
A max 1 1 0 | A max 1 1 1 | M e2 | A exp 0 0 | A max 1 2 0 | A exp 0 1 | B pack 2 | A max 1 2 1
A exp 0 2 | A max 1 3 0 | M up 6 | A max 1 3 1 | M up 7 | B max 0 0 0 | B max 0 0 1 | A exp 0 3
B max 0 1 0 | A pv 0 0 | B max 0 1 1 | B max 0 2 0 | B max 0 2 1 | A exp 0 4 | A pv 0 1 | B max 0 3 0
A mt 1 | B max 0 3 1 | A exp 0 5 | A exp 0 6 | M route2 | M down 0 0 | B mt 0 | A pv 0 2 | A exp 0 7
M down 0 1 | A exp 1 0 | B exp 0 0 | M down 0 2 | A pv 0 3 | A exp 1 1 | B max 1 0 0 | B max 1 0 1
B exp 0 1 | A exp 1 2 | A ut 0 0 | B exp 0 2 | B max 1 1 0 | B max 1 1 1 | B exp 0 3 | B max 1 2 0
B pv 0 0 | B pv 0 1 | B exp 0 4 | B max 1 2 1 | A0 load | A ut 0 1 | B exp 0 5 | A exp 1 3 | B max 1 3 0
B max 1 3 1 | B exp 0 6 | B exp 0 7 | M down 0 3 | B mt 1 | B pv 0 2 | A pv 1 0 | A exp 1 4 | M down 1 0
B exp 1 0 | A0 in | A pv 1 1 | B exp 1 1 | M down 1 1 | A exp 1 5 | A exp 1 6 | A0 qk | A pv 1 2
B pv 0 3 | A0 split | A exp 1 7 | M down 1 2 | A pv 1 3 | B ut 0 0 | A0 stow | A ut 1 0 | B exp 1 2
B exp 1 3 | A0 pack 0 | A ut 1 1 | M down 1 3 | A ot | B ut 0 1 | B pv 1 0 | B exp 1 4 | B pv 1 1
A0 pack 1 | B exp 1 5 | B exp 1 6 | B exp 1 7 | M ln2 | A0 pack 2 | A proj | A ln | B pv 1 2 | B pv 1 3
B ut 1 0 | B ut 1 1 | M out | M store | A out | A0 v | B ot | B proj | A0 xpb | B x12
""",
    "drain": """
B ln | M ln | B z | M z | B in | M in | B qk | M logits | M up 0 | M up 1 | M up 2 | M up 3 | B stow
M up 4 | B pack 0 | B pack 1 | B pack 2 | M route1 | M e2 | M up 5 | M route2 | M up 6 | M down 0 0
B max 0 0 0 | B max 0 0 1 | B max 0 1 0 | B max 0 1 1 | B max 0 2 0 | B max 0 2 1 | B max 0 3 0
B max 0 3 1 | B v | M down 0 1 | B mt 0 | M down 0 2 | B max 1 0 0 | M up 7 | B exp 0 0 | B max 1 0 1
B exp 0 1 | B max 1 1 0 | B max 1 1 1 | M down 0 3 | B exp 0 2 | B max 1 2 0 | B exp 0 3 | B max 1 2 1
B pv 0 0 | B max 1 3 0 | B exp 0 4 | B exp 0 5 | M down 1 0 | B pv 0 1 | B exp 0 6 | B max 1 3 1
B pv 0 2 | B exp 0 7 | B mt 1 | B pv 0 3 | M down 1 1 | B exp 1 0 | B ut 0 0 | B exp 1 1 | M down 1 2
B exp 1 2 | B ut 0 1 | B exp 1 3 | M down 1 3 | B pv 1 0 | B exp 1 4 | B exp 1 5 | B pv 1 1 | B exp 1 6
B exp 1 7 | M ln2 | B pv 1 2 | B pv 1 3 | B ut 1 0 | B ut 1 1 | M out | B ot | M store | B proj | B x12
""",
}


def turn_steps(kind):
    steps = [x.split() for x in TURNS[kind].replace("\n", "|").split("|") if x.strip()]
    return [tuple(int(w) if w.isdigit() else w for w in x) for x in steps]


SECTIONS = [
    (0, 1, {"A0": 0, "W0": 0}),
    (1, 2, {"A0": 0, "A": -1, "W1": 0}),
    (2, 3, {"A0": 0, "A": -1, "B": -2, "W2": 0}),
    (3, PAIRS, {"A0": 0, "A": -1, "B": -2, "M": -3}),
    (PAIRS, PAIRS + 1, {"A": -1, "B": -2, "M": -3}),
    (PAIRS + 1, PAIRS + 2, {"B": -2, "M": -3}),
    (PAIRS + 2, PAIRS + 3, {"M": -3}),
]


def d_units(s, step, *args):
    if step == "max":
        return 1 if s == "B" and args[2] == 0 else 2
    if step == "qk":
        return 4 if s == "A0" else 2
    return int(step in ("in", "ut", "proj", "down") or (s, step) == ("A0", "v"))


def a_units(s, step, *args):
    return int(step in ("exp", "pv", "up", "mt", "ot", "logits") or (s, step) == ("B", "v"))


def sections():
    out = []
    for lo, hi, offs in SECTIONS:
        steps = []
        for x in turn_steps("fill" if hi <= 3 else "full" if lo <= PAIRS else "drain"):
            if x[0] in offs:
                steps.append(x)
            if x == ("A0", "load") and "W0" in offs:
                steps.append(("W0", "load"))
            if x == ("A", "exp", 0, 3) and "W1" in offs:
                steps.append(("W1", "make"))
        if "W2" in offs:
            steps.insert(0, ("W2", "use"))
        d_at, a_at, nd, na = {}, {}, 0, 0
        for x in steps:
            d_at[x], a_at[x] = nd, na
            nd, na = nd + d_units(*x), na + a_units(*x)
        assert hi - lo == 1 or nd % D_SLOTS == 0 and na % A_SLOTS == 0
        out.append((lo, hi, offs, steps, d_at, a_at, nd, na))
    return out


PACKS = 16 * (3 + 3 * J)


def program(nc, x, w_a, b_cols, bv_row, proj_a, pb_row, ln1, w_b, proj_b, ln2, router, w1, w2,
            ident, rope, mask, ones_rows, out):
    f32, f16 = mybir.dt.float32, mybir.dt.float16
    ALU, ACT, AX = mybir.AluOpType, mybir.ActivationFunctionType, mybir.AxisListType

    x_v = x.rearrange("(n t p) c -> n p t c", t=TILES, p=P)
    out_v = out.rearrange("(n t p) c -> n p t c", t=TILES, p=P)

    ctx = ExitStack()
    with ctx:
        def sb(name, shape, dt=f32):
            return ctx.enter_context(nc.sbuf_tensor(name, shape, dt))

        def sem(name):
            return ctx.enter_context(nc.semaphore(name))

        hid = sb("hid", [P, NF, PAIR])
        wa_f = hid[:, 0:2, :].rearrange("p a n -> p (a n)")[:, 0:5 * C].rearrange("p (g c) -> p g c", g=5)
        wb_f = hid[:, 2, 0:3 * C].rearrange("p (g c) -> p g c", g=3)
        rt_f = hid[:, 3, 0:E]
        w1_f = hid[:, 4:4 + E * F // PAIR, :].rearrange("p a n -> p (a n)")
        wa = sb("wa", [P, 2, 5, C], f16)
        wb = sb("wb", [P, 2, 3, C], f16)
        w1s = sb("w1s", [P, 2, E * F], f16)
        w2s = sb("w2s", [P, NF, C])
        rts = sb("rts", [P, 2, E], f16)
        projs = {"A": sb("proj_as", [P, C]), "B": sb("proj_bs", [P, C])}
        bcol = sb("bcol", [P, 4])
        bv = sb("bv", [P, C])
        pb = sb("pb", [P, C])
        lnw = {"B": sb("ln1s", [P, 1]), "M": sb("ln2s", [P, 1])}
        idf = sb("idf", [P, P])
        big = sb("big", [P, P], f16)
        ropes = sb("ropes", [P, 2, T])
        masks = sb("masks", [P, P], f16)
        epsc = sb("epsc", [P, TILES])
        halfc = sb("halfc", [P, TILES])
        order = sb("order", [P, TILES, E])

        L = {}
        for s in "AB":
            L[s] = dict(
                xs=sb(f"xs{s}", [P, 2, PAIR], f16),
                qs=sb(f"qs{s}", [P, 2, 2, PAIR], f16),
                qp=sb(f"qp{s}", [P, QUADS, PAIR], f16),
                kz=sb(f"kz{s}", [P, QUADS, J, PAIR], f16),
                v=sb(f"v{s}", [P, TILES, H, 32]),
                mx=sb(f"mx{s}", [P, 2, 2, H]),
                mt=sb(f"mt{s}", [H, 2, T], f16),
                pt=sb(f"pt{s}", [P, 4, J, T]),
                u=sb(f"u{s}", [P, QUADS, T]),
                rec=sb(f"rec{s}", [P, 2, H]),
                o=sb(f"o{s}", [P, TILES, C]),
                scratch=nc.dram_tensor(f"scratch{s}", [2, 2, P, PAIR], f16, kind="Internal").ap(),
            )
            L[s]["ot"] = L[s]["o"][:, :, :].rearrange("p t c -> p (t c)")
        xin = sb("xin", [P, TILES, C])
        xpb = sb("xpb", [P, TILES, C])
        rot = sb("rot", [P, 4, PAIR])
        ya = xpb
        x1r = sb("x1r", [P, TILES, C])
        x1 = sb("x1", [P, TILES, C])
        zb = sb("zb", [P, TILES, C])
        x2 = sb("x2", [P, TILES, C])
        x12 = sb("x12", [P, TILES, C])
        zm = sb("zm", [P, TILES, C])
        xsm = sb("xsm", [P, 2, PAIR], f16)
        tmp = sb("tmp", [P, 2, 4, C])
        part = sb("part", [P, 2, C])
        half = sb("half", [P, C])
        acc = sb("acc", [P, TILES, C])
        yout = zm
        stats = {k: sb(f"stats{k}", [P, TILES, 6]) for k in ("a", "b", "m", "o")}
        mv = {k: sb(f"mv{k}", [P, TILES, 2]) for k in ("a", "b", "m", "o")}
        ve = {k: sb(f"ve{k}", [P, TILES]) for k in ("a", "b", "m", "o")}
        rstd = {k: sb(f"rstd{k}", [P, TILES]) for k in ("a", "b", "m", "o")}
        lg = sb("lg", [P, TILES, E])
        best = sb("best", [P, 2, TILES])
        eq = sb("eq", [P, TILES, E])
        turn_ = sb("turn_", [P, TILES])
        sel = sb("sel", [P, 2, TILES, E])
        rest = sb("rest", [P, TILES, E])
        diff = sb("diff", [P, TILES])
        ed = sb("ed", [P, TILES])
        den = sb("den", [P, TILES])
        wts = sb("wts", [P, 2, TILES])
        gsel = sb("gsel", [P, 2, TILES, E])
        gate = sb("gate", [P, TILES, E])

        d_ps = [ctx.enter_context(nc.psum_tensor(f"d_ps{i}", [P, 512], f32)) for i in range(D_SLOTS)]
        a_ps = [ctx.enter_context(nc.psum_tensor(f"a_ps{i}", [P, 1024], f32)) for i in range(A_SLOTS)]

        loaded = sem("loaded")
        loaded_b = sem("loaded_b")
        rows_set = sem("rows_set")
        wait_carried = sem("wait_carried")
        consts = sem("consts")
        zeroed = sem("zeroed")
        split_w = sem("split_w")
        d_full, d_free = sem("d_full"), sem("d_free")
        a_full, a_free = sem("a_full"), sem("a_free")
        counted = []

        def csem(name, start=1):
            counted.append((sem(name), start))
            return counted[-1][0]

        x_loaded = csem("x_loaded")
        xpb_done = csem("xpb_done")
        split_done = csem("split_done")
        out_stored = csem("out_stored")
        out_done = csem("out_done")
        x1_done = csem("x1_done")
        S = {}
        for s in "AB":
            S[s] = {k: csem(f"{k}_{s}") for k in (
                "stored",
                "packed",
            )}
            S[s]["mrows"] = [csem(f"mrows{b}_{s}") for b in range(2)]
        x12_done = csem("x12_done")
        masked = csem("masked")
        z_done = {s: csem(f"z_done{s}") for s in "BM"}
        stats_done = {k: csem(f"stats_done_{k}") for k in ("a", "b", "m", "o")}
        rstd_done = {k: csem(f"rstd_done_{k}") for k in ("a", "b", "m", "o")}
        diff_done, ed_done, gate_done = csem("diff_done"), csem("ed_done"), csem("gate_done")
        summed = csem("summed", 2)
        dve_link = {s: sem(f"dve_link_{s}") for s in ("A0", "A", "B", "M")}
        pool_link = {s: sem(f"pool_link_{s}") for s in ("A0", "A", "B", "M")}
        DVE_LINKS = {"A0": 1, "A": 5, "B": 9, "M": 18, "W0": 0, "W1": 0, "W2": 0}
        POOL_LINKS = {"A0": 4, "A": 1, "B": 1, "M": 18, "W0": 0, "W1": 0, "W2": 0}

        loads_a = ((wa_f, w_a), (idf[:, :], ident), (bcol[:, :], b_cols), (ropes[:, :, :], rope),
                   (bv[:, :], bv_row.partition_broadcast(P)), (pb[:, :], pb_row.partition_broadcast(P)),
                   (projs["A"][:, :], proj_a))
        loads_b = ((wb_f, w_b), (w1_f, w1), (rt_f, router), (masks[:, :], mask), (lnw["B"][:, :], ln1),
                   (projs["B"][:, :], proj_b), (lnw["M"][:, :], ln2), (w2s[:, :, :], w2))
        plan = sections()

        class Now:

            def __init__(self, i, section, base, links):
                lo, _, offs, _, self.d_at, self.a_at, nd, na = section
                self.turn = {s: Turn(i, o) for s, o in offs.items()}
                self.d = Ring(D_SLOTS, base[0] % D_SLOTS, (i - lo) * nd + base[0] if isinstance(i, int) else i * nd + (base[0] - lo * nd))
                self.a = Ring(A_SLOTS, base[1] % A_SLOTS, (i - lo) * na + base[1] if isinstance(i, int) else i * na + (base[1] - lo * na))
                self.first = "W0" in offs
                self.per, self.k = links, {s: 0 for s in offs}

            def d_done(self, *step, unit=0):
                return self.d.freed(self.d_at[step] + unit)

            def a_done(self, *step):
                return self.a.freed(self.a_at[step])

            def d_before(self):
                return self.d.base + D_SLOTS

            def a_before(self):
                return self.a.base + A_SLOTS

            def last_pair_used(self, s):
                return self.a_done("A", "pv", 1, QUADS - 1) if s == "A" and "A" in self.turn else self.a_before()

            def link(self, s):
                self.k[s] += 1
                return self.turn[s].raw(self.per[s], self.k[s])

            def end(self):
                for s, k in self.k.items():
                    assert self.per is None or k == self.per[s], (s, k, self.per[s])

        def walk(eng, do, links=None):
            base = [0, 0]
            for section in plan:
                lo, hi, _, steps, _, _, nd, na = section

                def turn(i):
                    now = Now(i, section, tuple(base), links)
                    for step in steps:
                        do(now, *step)
                    now.end()
                if hi - lo == 1:
                    turn(lo)
                else:
                    with eng.Fori(lo, hi) as i:
                        turn(i)
                base[0] += (hi - lo) * nd
                base[1] += (hi - lo) * na

        block = ctx.enter_context(nc.Block())

        @block.sync
        def _(sp):
            for dst, src in loads_a:
                sp.dma_start(dst, src).then_inc(loaded, 16)

            def constant_rows(n, s):
                sp.wait_ge(zeroed, n)
                sp.dma_start(L[s]["kz"][DATA:ROWS, :, :, :], ones_rows).then_inc(rows_set, 16)

            def do(now, stage, step, *args):
                t = now.turn[stage]
                s = "A" if stage == "A0" else stage
                if (stage, step) == ("A0", "load"):
                    sp.wait_ge(d_free, now.d_before())
                    sp.sem_inc(wait_carried, 1)
                    sp.wait_ge(xpb_done, t(1, 0))
                    sp.sem_inc(wait_carried, 1)
                    sp.dma_start(xin[:, :, :], x_v[t.index(), :, :, :]).then_inc(x_loaded, 16)
                    if now.first:
                        constant_rows(1, "A")
                if (stage, step) == ("W0", "load"):
                    for dst, src in loads_b:
                        sp.dma_start(dst, src).then_inc(loaded_b, 16)
                if (stage, step) == ("W1", "make"):
                    constant_rows(2, "B")
                if step == "stow":
                    B, Z = L[s], S[s]
                    sp.wait_ge(Z["packed"], t(PACKS, 0))
                    sp.sem_inc(wait_carried, 1)
                    for w in range(2):
                        if s == "A":
                            sp.wait_ge(split_done, t(2, w + 1))
                        else:
                            sp.wait_ge(d_free, now.d_done("B", "qk", unit=w))
                        sp.dma_start(B["scratch"][w].rearrange("h p n -> p h n"), B["qs"][:, w, :, :]).then_inc(Z["stored"], 16)
                if step == "pack":
                    c, = args
                    B, Z = L[s], S[s]
                    if c == 0:
                        sp.wait_ge(a_free, now.last_pair_used(s))
                        sp.sem_inc(wait_carried, 1)
                        sp.wait_ge(Z["stored"], t(32, 32))
                    h_q, h_k = ((0, 0), (0, 1), (1, 0))[c]
                    sp.dma_start(B["qp"][32 * c:32 * c + 32, :, :],
                                 B["scratch"][0][h_q].rearrange("(q r) n -> r q n", q=QUADS)).then_inc(Z["packed"], 16)
                    for j in range(J):
                        r = 32 * c + HD * j
                        sp.dma_start(B["kz"][r:r + HD, :, j, :],
                                     B["scratch"][1][h_k].rearrange("(q j d) n -> j d q n", q=QUADS, j=J)[j]).then_inc(Z["packed"], 16)
                if step == "mt":
                    b, = args
                    sp.wait_ge(a_free, now.a_done(s, "mt", b))
                    sp.dma_start(L[s]["qp"][DATA:ROWS, :, b * T:(b + 1) * T],
                                 L[s]["mt"][:, b, :].unsqueeze(1).to_broadcast([H, QUADS, T])).then_inc(S[s]["mrows"][b], 16)
                if step == "store":
                    sp.wait_ge(out_done, t(1, 1))
                    sp.sem_inc(wait_carried, 1)
                    sp.dma_start(out_v[t.index(), :, :, :], yout[:, :, :]).then_inc(out_stored, 16)

            for q, start in counted[0::4]:
                sp.sem_inc(q, start)
            walk(sp, do)
            sp.wait_ge(out_stored, 1 + 16 * PAIRS)

        @block.gpsimd
        def _(pool):
            for q, start in counted[1::4]:
                pool.sem_inc(q, start)
            pool.memset(L["A"]["v"][:, :, :, :], 0.0).then_inc(consts, 1)
            pool.wait_ge(consts, 1)
            pool.memset(L["A"]["v"][:, :, :, HD:HD + 1], 1.0).then_inc(consts, 1)
            pool.wait_ge(loaded, 16 * len(loads_a))

            def do(now, stage, step, *args):
                t = now.turn[stage]
                s = "A" if stage == "A0" else stage

                if stage == "W1":
                    pool.memset(epsc[:, :], EPS).then_inc(consts, 1)
                    pool.memset(halfc[:, :], -0.5).then_inc(consts, 1)
                    for e in range(E):
                        pool.memset(order[:, :, e:e + 1], float(E - e))
                    pool.memset(L["B"]["v"][:, :, :, :], 0.0).then_inc(consts, 1)
                    pool.wait_ge(consts, 5)
                    pool.memset(L["B"]["v"][:, :, :, HD:HD + 1], 1.0).then_inc(consts, 1)
                    pool.tensor_scalar(big[:, :], idf[:, :], DIAG, 0.0, ALU.mult, ALU.add).then_inc(consts, 1)

                def rsqrt(k):
                    pool.wait_ge(stats_done[k], t(1, 1))
                    pool.tensor_tensor(ve[k][:, :], mv[k][:, :, 1], epsc[:, :], ALU.add).then_inc(pool_link[stage], 1)
                    pool.wait_ge(pool_link[stage], now.link(stage))
                    pool.tensor_tensor(rstd[k][:, :], ve[k][:, :], halfc[:, :], ALU.pow).then_inc(rstd_done[k], 1)

                if step == "xpb":
                    pool.wait_ge(x_loaded, t(16, 16))
                    pool.wait_ge(x1_done, t(1, 0))
                    pool.tensor_tensor(xpb[:, :, :], xin[:, :, :], pb[:, :].unsqueeze(1).to_broadcast([P, TILES, C]), ALU.add).then_inc(xpb_done, 1)
                if step == "split":
                    for w in range(2):
                        pool.wait_ge(d_free, now.d_done("A0", "qk", unit=2 * w + 1))
                        pool.wait_ge(S["A"]["stored"], t(32, 0))
                        pool.tensor_tensor(L["A"]["qs"][:, w, 0, :], rot[:, 2 * w, :], rot[:, 2 * w + 1, :], ALU.add).then_inc(pool_link["A0"], 1)
                        pool.wait_ge(pool_link["A0"], now.link("A0"))
                        pool.tensor_tensor(rot[:, 2 * w, :], rot[:, 2 * w, :], rot[:, 2 * w + 1, :], ALU.add).then_inc(pool_link["A0"], 1)
                        pool.wait_ge(pool_link["A0"], now.link("A0"))
                        pool.tensor_tensor(L["A"]["qs"][:, w, 1, :], rot[:, 2 * w, :], L["A"]["qs"][:, w, 0, :], ALU.subtract).then_inc(split_done, 1)
                if (s, step) == ("A", "ln"):
                    rsqrt("a")
                if (s, step) == ("B", "ln"):
                    rsqrt("b")
                if (s, step) == ("M", "ln"):
                    rsqrt("m")
                if (s, step) == ("M", "ln2"):
                    rsqrt("o")
                if step == "x12":
                    pool.wait_ge(d_free, now.d_done("B", "proj"))
                    pool.tensor_tensor(x12[:, :, :], x2[:, :, :], x1r[:, :, :], ALU.add).then_inc(x12_done, 1)
                if (s, step) == ("B", "exp"):
                    b, u = args
                    kt = u % 2
                    pool.wait_ge(a_free, now.a_done("B", "exp", b, u))
                    pool.sem_inc(wait_carried, 1)
                    v = L["B"]["pt"][:, u % 4, :, kt * P:(kt + 1) * P]
                    pool.affine_select(out=v, in_=v, pattern=[[0, J], [1, P]], compare_op=ALU.is_ge, fill=0.0,
                                       base=0, channel_multiplier=-1).then_inc(masked, 1)
                if (s, step) == ("M", "down"):
                    g, tile = args
                    n = TILES * g + tile
                    pool.wait_ge(d_free, now.d_done("M", "down", g, tile))
                    if n == 0:
                        pool.wait_ge(out_done, t(1, 0))
                        pool.wait_ge(x12_done, t(1, 1))
                    tm = tmp[:, n % 2]
                    pool.tensor_tensor(part[:, :, :], tm[:, 0:2, :], tm[:, 2:4, :], ALU.add).then_inc(pool_link["M"], 1)
                    pool.wait_ge(pool_link["M"], now.link("M"))
                    pool.tensor_tensor(half[:, :], part[:, 0, :], part[:, 1, :], ALU.add).then_inc(pool_link["M"], 1)
                    pool.wait_ge(pool_link["M"], now.link("M"))
                    pool.tensor_tensor(acc[:, tile, :], half[:, :], x12[:, tile, :] if g == 0 else acc[:, tile, :], ALU.add).then_inc(summed, 1)
                    pool.wait_ge(summed, t(8, n + 2))

            walk(pool, do, POOL_LINKS)

        @block.scalar
        def _(act):
            for q, start in counted[2::4]:
                act.sem_inc(q, start)
            act.sem_inc(a_free, A_SLOTS)

            def do(now, stage, step, *args):
                t = now.turn[stage]
                s = "A" if stage == "A0" else stage
                if step == "exp":
                    b, u = args
                    B = L[s]
                    slot, count = now.a.next()
                    act.wait_ge(a_full, count)
                    if s == "B" and u % 2:
                        dst, src = B["pt"][:, u % 4, :, P:T], a_ps[slot][:, 0:J * P].rearrange("p (j n) -> p j n", j=J)
                    else:
                        dst, src = B["pt"][:, u % 4, :, :], a_ps[slot][:, :].rearrange("p (j n) -> p j n", j=J)
                    act.activation(dst, src, ACT.Exp, scale=SCALE).then_inc(a_free, 1)
                if step == "pv":
                    b, q = args
                    B = L[s]
                    slot, count = now.a.next()
                    act.wait_ge(a_full, count)
                    act.wait_ge(d_free, now.d_done(s, "ut", 0, 1) if b else now.d_before())
                    act.activation(B["u"][:, q, :], a_ps[slot][:, 0:T], ACT.Copy).then_inc(a_free, 1)
                if (s, step) == ("B", "v"):
                    slot, count = now.a.next()
                    act.wait_ge(a_full, count)
                    act.activation(L["B"]["v"][:, :, :, 0:HD], a_ps[slot][:, 0:PAIR].rearrange("p (t h d) -> p t h d", t=TILES, d=HD),
                                   ACT.Copy).then_inc(a_free, 1)
                if step == "mt":
                    b, = args
                    for bb in range(2):
                        act.wait_ge(S[s]["mrows"][bb], t(16, 0))
                    slot, count = now.a.next()
                    act.wait_ge(a_full, count)
                    act.activation(L[s]["mt"][:, b, :], a_ps[slot][0:H, 0:T], ACT.Copy, scale=-1.0 / MSCALE).then_inc(a_free, 1)
                if step == "ot":
                    slot, count = now.a.next()
                    act.wait_ge(a_full, count)
                    act.activation(L[s]["ot"], a_ps[slot][:, 0:PAIR], ACT.Copy).then_inc(a_free, 1)
                if step == "logits":
                    slot, count = now.a.next()
                    act.wait_ge(a_full, count)
                    act.wait_ge(gate_done, t(1, 0))
                    act.activation(lg[:, :, :], a_ps[slot][:, 0:TILES * E].rearrange("p (t e) -> p t e", e=E), ACT.Copy).then_inc(a_free, 1)
                if step == "e2":
                    act.wait_ge(diff_done, t(1, 1))
                    act.wait_ge(gate_done, t(1, 0))
                    act.activation(ed[:, :], diff[:, :], ACT.Exp).then_inc(ed_done, 1)
                if step == "up":
                    c, = args
                    slot, count = now.a.next()
                    act.wait_ge(a_full, count)
                    if c == 0:
                        act.wait_ge(d_free, now.d_before())
                    act.activation(hid[:, 2 * c:2 * c + 2, :], a_ps[slot][:, :].rearrange("p (c n) -> p c n", c=2), ACT.Gelu).then_inc(a_free, 1)

            walk(act, do)

        @block.tensor
        def _(pe):
            for q, start in counted[3::4]:
                pe.sem_inc(q, start)
            pe.wait_ge(loaded, 16 * len(loads_a))
            pe.wait_ge(split_w, 2)

            def three(dst, wide, moving):
                for n, (a, b) in enumerate(((0, 0), (1, 0), (0, 1))):
                    last = pe.matmul(dst, wide(a), moving(b), start=n == 0, stop=n == 2)
                return last

            def turned(dst, src):
                for i in range(TILES):
                    last = pe.transpose(dst[:, i * P:(i + 1) * P], src[:, i, :], idf[:, :])
                return last

            def do(now, stage, step, *args):
                t = now.turn[stage]
                s = "A" if stage == "A0" else stage
                if stage == "W2":
                    pe.wait_ge(loaded_b, 16 * len(loads_b))
                    pe.wait_ge(rows_set, 32)
                    pe.wait_ge(consts, 7)
                    pe.wait_ge(split_w, 8)
                if step == "in":
                    if s == "A":
                        pe.wait_ge(x_loaded, t(16, 16))
                    else:
                        pe.wait_ge(z_done[s], t(1, 1))
                    slot, count = now.d.next()
                    pe.wait_ge(d_free, count)
                    turned(d_ps[slot], {"A": xin, "B": zb, "M": zm}[s]).then_inc(d_full, 1)
                if step in ("qk", "v"):
                    xs, w, n_t = (L["A"]["xs"], wa, 4) if s == "A" else (L["B"]["xs"], wb, 2)
                if step == "qk":
                    pe.wait_ge(d_free, now.d_done(stage, "in"))
                    for g in range(n_t):
                        slot, count = now.d.next()
                        pe.wait_ge(d_free, count)
                        three(d_ps[slot][:, :], lambda a: w[:, a, g, :], lambda b: xs[:, b, :]).then_inc(d_full, 1)
                if step == "v":
                    if s == "B":
                        pe.wait_ge(d_free, now.d_done("B", "in"))
                    slot, count = now.d.next() if s == "A" else now.a.next()
                    pe.wait_ge(d_free if s == "A" else a_free, count)
                    dst = (d_ps if s == "A" else a_ps)[slot]
                    for i in range(TILES):
                        last = three(dst[:, i * P:(i + 1) * P], lambda a: xs[:, a, i * P:(i + 1) * P],
                                     lambda b: w[:, b, n_t, :])
                    last.then_inc(d_full if s == "A" else a_full, 1)
                if step == "max":
                    b, q, qt = args
                    B = L[s]
                    if b == 0 and q == 0:
                        pe.wait_ge(S[s]["packed"], t(PACKS, PACKS))
                        pe.wait_ge(rows_set, 16 if s == "A" else 32)
                    at = b * T + qt * P
                    wide = B["qp"][0:DATA, q, at:at + P]
                    if s == "B" and qt == 0:
                        slot, count = now.d.next()
                        pe.wait_ge(d_free, count)
                        pe.matmul(d_ps[slot][:, :], wide, B["kz"][0:DATA, q, :, b * T:b * T + P], start=True, stop=False)
                        pe.matmul(d_ps[slot][:, :], big[:, :], masks[:, :].unsqueeze(1).to_broadcast([P, J, P]),
                                  start=False, stop=True).then_inc(d_full, 1)
                    else:
                        for h in range(2):
                            slot, count = now.d.next()
                            pe.wait_ge(d_free, count)
                            last = pe.matmul(d_ps[slot][:, :], wide, B["kz"][0:DATA, q, 2 * h:2 * h + 2, b * T:(b + 1) * T],
                                             start=True, stop=s == "A")
                            if s == "B":
                                last = pe.matmul(d_ps[slot][:, :].rearrange("p (j n) -> p j n", j=2)[:, :, P:T], big[:, :],
                                                 masks[:, :].unsqueeze(1).to_broadcast([P, 2, P]), start=False, stop=True)
                            last.then_inc(d_full, 1)
                if step == "mt":
                    b, = args
                    pe.wait_ge(d_free, now.d_done(s, "max", b, QUADS - 1, 1, unit=1))
                    slot, count = now.a.next()
                    pe.wait_ge(a_free, count)
                    for qt in range(2):
                        last = pe.transpose(a_ps[slot][0:H, qt * P:(qt + 1) * P], L[s]["mx"][:, b, qt, :], idf[:, :])
                    last.then_inc(a_full, 1)
                if step == "exp":
                    b, u = args
                    B = L[s]
                    q, kt = u // 2, u % 2
                    if u == 0:
                        pe.wait_ge(S[s]["mrows"][b], t(16, 16))
                    slot, count = now.a.next()
                    pe.wait_ge(a_free, count)
                    first = P if s == "B" and kt else 0
                    n = T - first
                    for j in range(J):
                        last = pe.matmul(a_ps[slot][:, j * n:(j + 1) * n], B["kz"][0:ROWS, q, j, b * T + kt * P:b * T + (kt + 1) * P],
                                         B["qp"][0:ROWS, q, b * T + first:(b + 1) * T], start=True, stop=True)
                    last.then_inc(a_full, 1)
                if step == "pv":
                    b, q = args
                    B = L[s]
                    if b == 0 and q == 0:
                        if s == "A":
                            pe.wait_ge(d_free, now.d_before())
                        else:
                            pe.wait_ge(a_free, now.a_done("B", "v"))
                    slot, count = now.a.next()
                    pe.wait_ge(a_free, count)
                    for kt in range(2):
                        u = 2 * q + kt
                        if s == "A":
                            pe.wait_ge(a_free, now.a_done("A", "exp", b, u))
                        else:
                            pe.wait_ge(masked, t(16, 8 * b + u + 1))
                        first = P if s == "B" and kt else 0
                        for j in range(J):
                            last = pe.matmul(a_ps[slot][32 * j:32 * j + 32, first:T], B["v"][:, 2 * b + kt, J * q + j, :],
                                             B["pt"][:, u % 4, j, first:T], start=kt == 0, stop=kt == 1)
                    last.then_inc(a_full, 1)
                if step == "ut":
                    b, qt = args
                    pe.wait_ge(a_free, now.a_done(s, "pv", b, 3))
                    slot, count = now.d.next()
                    pe.wait_ge(d_free, count)
                    for q in range(QUADS):
                        last = pe.transpose(d_ps[slot][:, q * P:(q + 1) * P], L[s]["u"][:, q, qt * P:(qt + 1) * P], idf[:, :])
                    last.then_inc(d_full, 1)
                if step == "ot":
                    pe.wait_ge(d_free, now.d_done(s, "ut", 1, 1))
                    slot, count = now.a.next()
                    pe.wait_ge(a_free, count)
                    turned(a_ps[slot], L[s]["o"]).then_inc(a_full, 1)
                if step == "proj":
                    pe.wait_ge(a_free, now.a_done(s, "ot"))
                    slot, count = now.d.next()
                    pe.wait_ge(d_free, count)
                    for i in range(TILES):
                        last = pe.matmul(d_ps[slot][:, i * P:(i + 1) * P], L[s]["ot"][:, i * P:(i + 1) * P], projs[s][:, :],
                                         start=True, stop=True)
                    last.then_inc(d_full, 1)
                if step == "logits":
                    pe.wait_ge(d_free, now.d_done("M", "in"))
                    slot, count = now.a.next()
                    pe.wait_ge(a_free, count)
                    for i in range(TILES):
                        last = three(a_ps[slot][:, i * E:(i + 1) * E], lambda a: xsm[:, a, i * P:(i + 1) * P], lambda b: rts[:, b, :])
                    last.then_inc(a_full, 1)
                if step == "up":
                    c, = args
                    if c == 0:
                        pe.wait_ge(d_free, now.d_done("M", "in"))
                    slot, count = now.a.next()
                    pe.wait_ge(a_free, count)
                    for k in range(2):
                        f = 2 * c + k
                        last = three(a_ps[slot][:, k * PAIR:(k + 1) * PAIR], lambda a: w1s[:, a, f * P:(f + 1) * P], lambda b: xsm[:, b, :])
                    last.then_inc(a_full, 1)
                if step == "down":
                    g, tile = args
                    if tile == 0:
                        pe.wait_ge(a_free, now.a_done("M", "up", 4 * g + 3))
                    slot, count = now.d.next()
                    pe.wait_ge(d_free, count)
                    for e in range(4):
                        for k in range(2):
                            f = 2 * (4 * g + e) + k
                            last = pe.matmul(d_ps[slot][:, e * C:(e + 1) * C], hid[:, f, tile * P:(tile + 1) * P], w2s[:, f, :],
                                             start=k == 0, stop=k == 1)
                    last.then_inc(d_full, 1)

            walk(pe, do)

        @block.vector
        def _(dve):
            dve.sem_inc(d_free, D_SLOTS)
            dve.memset(L["A"]["kz"][:, :, :, :], 0.0).then_inc(zeroed, 1)
            dve.wait_ge(loaded, 16 * len(loads_a))

            def split(f, highs, lows, k):
                dve.tensor_copy(highs, f).then_inc(split_w, 1)
                dve.wait_ge(split_w, 2 * k - 1)
                dve.tensor_tensor(lows, f, highs, ALU.subtract).then_inc(split_w, 1)

            split(wa_f, wa[:, 0, :, :], wa[:, 1, :, :], 1)
            dve.wait_ge(consts, 2)

            def ring(now):
                slot, count = now.d.next()
                dve.wait_ge(d_full, count)
                return d_ps[slot]

            def do(now, stage, step, *args):
                t = now.turn[stage]
                s = "A" if stage == "A0" else stage
                link = dve_link.get(stage)

                if stage == "W1":
                    dve.memset(L["B"]["kz"][:, :, :, :], 0.0).then_inc(zeroed, 1)
                    dve.wait_ge(loaded_b, 16 * len(loads_b))
                    split(wb_f, wb[:, 0, :, :], wb[:, 1, :, :], 2)
                    split(w1_f, w1s[:, 0, :], w1s[:, 1, :], 3)
                    split(rt_f, rts[:, 0, :], rts[:, 1, :], 4)
                    dve.wait_ge(consts, 7)

                def stats_of(k, src):
                    for i in range(TILES):
                        last = dve.bn_stats(stats[k][:, i, :], src[:, i, :])
                    last.then_inc(link, 1)
                    dve.wait_ge(link, now.link(stage))
                    dve.sem_inc(wait_carried, 1)
                    for i in range(TILES):
                        last = dve.bn_aggr(mv[k][:, i, :], stats[k][:, i, :])
                    last.then_inc(stats_done[k], 1)

                def normalised(k, dst, src, done):
                    dve.wait_ge(rstd_done[k], t(1, 1))
                    for i in range(TILES):
                        last = dve.tensor_scalar(dst[:, i, :], src[:, i, :], mv[k][:, i, 0:1], rstd[k][:, i:i + 1], ALU.subtract, ALU.mult)
                    last.then_inc(done, 1)

                if step == "in":
                    xs = xsm if s == "M" else L[s]["xs"]
                    if s == "M":
                        dve.wait_ge(a_free, now.a_before())
                    ps = ring(now)
                    if s == "A":
                        dve.tensor_copy(xs[:, 0, :], ps[:, :]).then_inc(link, 1)
                        dve.wait_ge(link, now.link(stage))
                        dve.tensor_tensor(xs[:, 1, :], ps[:, :], xs[:, 0, :], ALU.subtract).then_inc(d_free, 1)
                    else:
                        dve.tensor_scalar(xs[:, 0, :], ps[:, :], lnw[s][:, 0:1], None, ALU.mult).then_inc(link, 1)
                        dve.wait_ge(link, now.link(stage))
                        dve.scalar_tensor_tensor(xs[:, 1, :], ps[:, :], lnw[s][:, 0:1], xs[:, 0, :], ALU.mult, ALU.subtract).then_inc(d_free, 1)
                if stage == "A0" and step == "qk":
                    dve.wait_ge(split_done, t(2, 0))
                    for g in range(4):
                        ps = ring(now)
                        dve.scalar_tensor_tensor(rot[:, g, :].rearrange("p (b n) -> p b n", b=2), ps[:, :].rearrange("p (b n) -> p b n", b=2),
                                                 bcol[:, g:g + 1], ropes[:, g % 2, :].unsqueeze(1).to_broadcast([P, 2, T]),
                                                 ALU.add, ALU.mult).then_inc(d_free, 1)
                if (s, step) == ("B", "qk"):
                    dve.wait_ge(S["B"]["stored"], t(32, 0))
                    for g in range(2):
                        ps = ring(now)
                        qs = L["B"]["qs"]
                        dve.tensor_copy(qs[:, g, 0, :], ps[:, :]).then_inc(link, 1)
                        dve.wait_ge(link, now.link(stage))
                        dve.tensor_tensor(qs[:, g, 1, :], ps[:, :], qs[:, g, 0, :], ALU.subtract).then_inc(d_free, 1)
                if (stage, step) == ("A0", "v"):
                    dve.wait_ge(a_free, now.last_pair_used(s))
                    ps = ring(now)
                    v = L[s]["v"]
                    for i in range(TILES):
                        last = dve.tensor_tensor(v[:, i, :, 0:HD], ps[:, i * P:(i + 1) * P].rearrange("p (h d) -> p h d", d=HD),
                                                 bv[:, :].rearrange("p (h d) -> p h d", d=HD), ALU.add)
                    last.then_inc(d_free, 1)
                if step == "max":
                    b, q, qt = args
                    mx = L[s]["mx"]
                    if s == "B" and qt == 0:
                        ps = ring(now)
                        dve.tensor_reduce(mx[:, b, 0, J * q:J * q + J], ps[:, :].rearrange("p (j n) -> p j n", j=J), AX.X, ALU.max).then_inc(d_free, 1)
                    else:
                        for h in range(2):
                            ps = ring(now)
                            at = J * q + 2 * h
                            dve.tensor_reduce(mx[:, b, qt, at:at + 2], ps[:, :].rearrange("p (j n) -> p j n", j=2), AX.X, ALU.max).then_inc(d_free, 1)
                if step == "ut":
                    b, qt = args
                    B = L[s]
                    ps = ring(now)
                    v = ps[:, :].rearrange("p (h r) -> p h r", r=32)
                    dve.reciprocal(B["rec"][:, qt, :], v[:, :, HD]).then_inc(link, 1)
                    dve.wait_ge(link, now.link(stage))
                    dve.tensor_tensor(B["o"][:, 2 * b + qt, :].rearrange("p (h d) -> p h d", d=HD), v[:, :, 0:HD],
                                      B["rec"][:, qt, :].unsqueeze(2).to_broadcast([P, H, HD]), ALU.mult).then_inc(d_free, 1)
                if step == "proj":
                    if s == "A":
                        dve.wait_ge(xpb_done, t(1, 1))
                        dst, res = ya, xpb
                    else:
                        dve.wait_ge(x12_done, t(1, 0))
                        dst, res = x2, x1r
                    ps = ring(now)
                    dve.tensor_tensor(dst[:, :, :], ps[:, :].rearrange("p (t c) -> p t c", t=TILES), res[:, :, :], ALU.add).then_inc(d_free, 1)
                if (s, step) == ("A", "ln"):
                    dve.wait_ge(d_free, now.d_done("A", "proj"))
                    stats_of("a", ya)
                if (s, step) == ("A", "out"):
                    normalised("a", x1, ya, x1_done)
                if (s, step) == ("B", "ln"):
                    dve.wait_ge(x1_done, t(1, 1))
                    stats_of("b", x1)
                    dve.wait_ge(x12_done, t(1, 0))
                    dve.tensor_copy(x1r[:, :, :], x1[:, :, :]).then_inc(link, 1)
                    dve.wait_ge(link, now.link(stage))
                if (s, step) == ("B", "z"):
                    normalised("b", zb, x1, z_done["B"])
                if (s, step) == ("M", "ln"):
                    dve.wait_ge(d_free, now.d_before())
                    stats_of("m", x2)
                if (s, step) == ("M", "z"):
                    dve.wait_ge(out_stored, t(16, 0))
                    normalised("m", zm, x2, z_done["M"])
                def wide(ap):
                    return ap.unsqueeze(2).to_broadcast([P, TILES, E])

                def choose(n, src):
                    dve.tensor_reduce(best[:, n, :], src, AX.X, ALU.max).then_inc(link, 1)
                    dve.wait_ge(link, now.link(stage))
                    dve.tensor_tensor(eq[:, :, :], src, wide(best[:, n, :]), ALU.is_ge).then_inc(link, 1)
                    dve.wait_ge(link, now.link(stage))
                    dve.tensor_tensor(eq[:, :, :], eq[:, :, :], order[:, :, :], ALU.mult).then_inc(link, 1)
                    dve.wait_ge(link, now.link(stage))
                    dve.tensor_reduce(turn_[:, :], eq[:, :, :], AX.X, ALU.max).then_inc(link, 1)
                    dve.wait_ge(link, now.link(stage))
                    dve.tensor_tensor(sel[:, n, :, :], eq[:, :, :], wide(turn_[:, :]), ALU.is_equal).then_inc(link, 1)
                    dve.wait_ge(link, now.link(stage))

                if step == "route1":
                    dve.wait_ge(a_free, now.a_done("M", "logits"))
                    choose(0, lg[:, :, :])
                    dve.scalar_tensor_tensor(rest[:, :, :], sel[:, 0, :, :], -3.0e38, lg[:, :, :], ALU.mult, ALU.add).then_inc(link, 1)
                    dve.wait_ge(link, now.link(stage))
                    choose(1, rest[:, :, :])
                    dve.tensor_tensor(diff[:, :], best[:, 1, :], best[:, 0, :], ALU.subtract).then_inc(diff_done, 1)
                if step == "route2":
                    dve.wait_ge(ed_done, t(1, 1))
                    dve.tensor_scalar(den[:, :], ed[:, :], 1.0, None, ALU.add).then_inc(link, 1)
                    dve.wait_ge(link, now.link(stage))
                    dve.reciprocal(wts[:, 0, :], den[:, :]).then_inc(link, 1)
                    dve.wait_ge(link, now.link(stage))
                    dve.tensor_tensor(wts[:, 1, :], wts[:, 0, :], ed[:, :], ALU.mult).then_inc(link, 1)
                    dve.wait_ge(link, now.link(stage))
                    for n in range(2):
                        last = dve.tensor_tensor(gsel[:, n, :, :], sel[:, n, :, :], wide(wts[:, n, :]), ALU.mult)
                    last.then_inc(link, 1)
                    dve.wait_ge(link, now.link(stage))
                    dve.tensor_tensor(gate[:, :, :], gsel[:, 0, :, :], gsel[:, 1, :, :], ALU.add).then_inc(gate_done, 1)
                    dve.wait_ge(gate_done, t(1, 1))
                if step == "down":
                    g, tile = args
                    n = TILES * g + tile
                    dve.wait_ge(summed, t(8, n))
                    ps = ring(now)
                    dve.tensor_tensor(tmp[:, n % 2], ps[:, :].rearrange("p (e c) -> p e c", e=4),
                                      gate[:, tile, 4 * g:4 * g + 4].unsqueeze(2).to_broadcast([P, 4, C]), ALU.mult).then_inc(d_free, 1)
                if (s, step) == ("M", "ln2"):
                    dve.wait_ge(summed, t(8, 8 + 1))
                    stats_of("o", acc)
                if (s, step) == ("M", "out"):
                    normalised("o", yout, acc, out_done)

            walk(dve, do, DVE_LINKS)


_INS = ["x", "w_a", "b_cols", "bv_row", "proj_a", "pb_row", "ln1", "w_b", "proj_b", "ln2", "router", "w1", "w2",
        "ident", "rope", "mask", "ones_rows"]


def constants():
    pos = np.arange(T, dtype=np.float32)
    inv = (1.0 / np.float32(10000.0) ** (np.arange(0, HD, 2, dtype=np.float32) / np.float32(HD))).astype(np.float32)
    freqs = pos[None, :] * inv[:, None]
    cos, sin = np.cos(freqs), np.sin(freqs)
    d = np.arange(P) % HD
    sign = np.where(d % 2 == 0, -1.0, 1.0)[:, None].astype(np.float32)
    rope = np.stack([cos[d // 2], sin[d // 2] * sign], axis=1).astype(np.float32)
    q, k = np.arange(P)[:, None], np.arange(P)[None, :]
    mask = np.where(k > q, -MASKED, 0.0).astype(np.float16)
    rows = np.zeros((H, QUADS, J, PAIR), np.float16)
    for h in range(H):
        rows[h, h // J, h % J, :] = MSCALE
    return {"ident": np.eye(P, dtype=np.float32), "rope": rope, "mask": mask, "ones_rows": rows}


def kernel(L0_attn_x, L0_attn_qkv_w, L0_attn_qkv_b, L0_attn_proj_w, L0_attn_proj_b, L0_ffn_ln1_w,
           L0_ffn_c_attn_w, L0_ffn_c_proj_w, L0_ffn_ln2_w, L0_ffn_router_w, L0_ffn_w1, L0_ffn_w2):
    import concourse.bacc as bacc
    from concourse.bass_utils import run_bass_kernel_spmd

    swapped = np.arange(C) ^ 1
    w = np.asarray(L0_attn_qkv_w).reshape(3, C, C)
    bias = np.asarray(L0_attn_qkv_b).reshape(3, C)
    arrays = {
        "x": np.asarray(L0_attn_x).reshape(SEQ * T, C),
        "w_a": np.stack([w[0].T, w[0][swapped].T, w[1].T, w[1][swapped].T, w[2].T], axis=1),
        "b_cols": np.stack([bias[0], bias[0][swapped], bias[1], bias[1][swapped]], axis=1),
        "bv_row": bias[2],
        "proj_a": np.asarray(L0_attn_proj_w).T,
        "pb_row": np.asarray(L0_attn_proj_b),
        "ln1": np.asarray(L0_ffn_ln1_w).reshape(C, 1),
        "w_b": np.asarray(L0_ffn_c_attn_w).reshape(C, 3, C),
        "proj_b": np.asarray(L0_ffn_c_proj_w),
        "ln2": np.asarray(L0_ffn_ln2_w).reshape(C, 1),
        "router": np.asarray(L0_ffn_router_w),
        "w1": np.asarray(L0_ffn_w1),
        "w2": np.asarray(L0_ffn_w2).reshape(NF, P, C).transpose(1, 0, 2),
        **constants(),
    }
    arrays = {k: np.ascontiguousarray(v) for k, v in arrays.items()}
    nc = bacc.Bacc("TRN2", target_bir_lowering=False, num_devices=1)
    args = [nc.dram_tensor(f"in_{k}", arrays[k].shape, mybir.dt.from_np(arrays[k].dtype), kind="ExternalInput").ap() for k in _INS]
    out = nc.dram_tensor("out_0", (SEQ * T, C), mybir.dt.float32, kind="ExternalOutput").ap()
    program(nc, *args, out)
    r = run_bass_kernel_spmd(nc, [{f"in_{k}": arrays[k] for k in _INS}], core_ids=[0])
    return r.results[0]["out_0"].reshape(SEQ, T, C)
```
